# Optimizing a Trainium2 kernel written in Bass

```python
import numpy as np
import jax
import jax.numpy as jnp

def _softmax(x, axis=-1):
    return jax.nn.softmax(x, axis=axis)

def _gelu(x):
    return jax.nn.gelu(x, approximate=True)

def _silu(x):
    return jax.nn.silu(x)

def _sigmoid(x):
    return jax.nn.sigmoid(x)

def _layernorm(x, axis=-1, eps=1e-05):
    m = jnp.mean(x, axis=axis, keepdims=True)
    v = jnp.var(x, axis=axis, keepdims=True)
    return (x - m) / jnp.sqrt(v + eps)

def _scatter_add(tgt, idx, src, axis=0):
    return tgt.at[idx].add(src)

def _segment_sum(src, seg, n):
    return jax.ops.segment_sum(src, seg, n)
kernel_name = 'mk_recurrent_d2_jaxref_r8_50f9f7'

def setup_inputs(seed: int=0):
    np.random.seed(seed)
    _w = jnp.asarray

    def _L0_attn_setup():
        import jax, jax.numpy as jnp
        import numpy as np
        import math
        N_EMBD = 256
        N_HEADS = 16
        HEAD_DIM = N_EMBD // N_HEADS
        CTX = 256

        def alibi_bias(seq_len: int, n_heads: int) -> jnp.ndarray:
            i = jnp.arange(seq_len)[:, None]
            j = jnp.arange(seq_len)[None, :]
            pos = jnp.where(j <= i, (j - i).astype(jnp.float32), 0.0)
            slopes = 2.0 ** (-8.0 / jnp.arange(1, n_heads + 1, dtype=jnp.float32))
            return slopes[:, None, None] * pos[None, :, :]

        def causal_mask(seq_len: int) -> jnp.ndarray:
            i = jnp.arange(seq_len)[:, None]
            j = jnp.arange(seq_len)[None, :]
            return jnp.where(j > i, -jnp.inf, 0.0).astype(jnp.float32)
        key = jax.random.key(seed)
        k_x, k_qkv, k_o = jax.random.split(key, 3)
        scale = 1.0 / math.sqrt(N_EMBD)
        x = jax.random.normal(k_x, (2, CTX, N_EMBD), dtype=jnp.float32)
        W_qkv = jax.random.normal(k_qkv, (N_EMBD, 3 * N_EMBD), dtype=jnp.float32) * scale
        W_o = jax.random.normal(k_o, (N_EMBD, N_EMBD), dtype=jnp.float32) * scale
        return {'x': x, 'W_qkv': W_qkv, 'W_o': W_o}
    _L0_attn_in = _L0_attn_setup()

    def _L0_ffn_setup():
        import jax, jax.numpy as jnp
        import numpy as np
        B, S, D, H = (4, 256, 256, 1024)

        def fwht(x):
            orig_shape = x.shape
            n = orig_shape[-1]
            x = x.reshape(-1, n)
            h = 1
            while h < n:
                xb = x.reshape(-1, n // (2 * h), 2, h)
                a = xb[:, :, 0, :]
                b = xb[:, :, 1, :]
                x = jnp.stack([a + b, a - b], axis=2).reshape(-1, n)
                h *= 2
            scale = jnp.asarray(1.0 / np.sqrt(n), dtype=x.dtype)
            return (x * scale).reshape(orig_shape)
        key = jax.random.key(seed)
        kx, k1, k2, k3 = jax.random.split(key, 4)
        x = jax.random.normal(kx, (B, S, D), dtype=jnp.float32)
        W1 = jax.random.normal(k1, (H, D), dtype=jnp.float32) * (1.0 / np.sqrt(D))
        W2 = jax.random.normal(k2, (D, H), dtype=jnp.float32) * (1.0 / np.sqrt(H))
        W3 = jax.random.normal(k3, (H, D), dtype=jnp.float32) * (1.0 / np.sqrt(D))
        return {'x': x, 'W1': W1, 'W2': W2, 'W3': W3}
    _L0_ffn_in = _L0_ffn_setup()

    def _L1_attn_setup():
        import jax, jax.numpy as jnp
        import numpy as np
        B, T, D_MODEL = (2, 256, 256)
        N_HEADS, D_HEAD = (16, 128)
        MAX_SEQ_LEN = 256
        LOGIT_SOFTCAP = 50.0
        EPS = 1e-06

        def precompute_rope(dim, max_seq_len, theta=10000.0):
            freqs = 1.0 / theta ** (np.arange(0, dim, 2, dtype=np.float32) / dim)
            t = np.arange(max_seq_len, dtype=np.float32)
            angles = np.outer(t, freqs)
            return (jnp.asarray(np.cos(angles)), jnp.asarray(np.sin(angles)))

        def rmsnorm(x, w):
            return x * jax.lax.rsqrt(jnp.mean(x * x, axis=-1, keepdims=True) + EPS) * w

        def apply_rope(x, cos, sin):
            n = x.shape[1]
            x1, x2 = (x[..., ::2], x[..., 1::2])
            c = cos[:n][None, :, None, :]
            s = sin[:n][None, :, None, :]
            out = jnp.stack([x1 * c - x2 * s, x1 * s + x2 * c], axis=-1)
            return out.reshape(x.shape)
        key = jax.random.key(seed)
        ks = jax.random.split(key, 6)
        x = jax.random.normal(ks[0], (B, T, D_MODEL), dtype=jnp.float32)
        wq = 0.02 * jax.random.normal(ks[1], (N_HEADS * D_HEAD, D_MODEL), dtype=jnp.float32)
        wk = 0.02 * jax.random.normal(ks[2], (N_HEADS * D_HEAD, D_MODEL), dtype=jnp.float32)
        wv = 0.02 * jax.random.normal(ks[3], (N_HEADS * D_HEAD, D_MODEL), dtype=jnp.float32)
        wo = 0.02 * jax.random.normal(ks[4], (D_MODEL, N_HEADS * D_HEAD), dtype=jnp.float32)
        q_norm_w = jnp.ones((D_HEAD,), dtype=jnp.float32)
        k_norm_w = jnp.ones((D_HEAD,), dtype=jnp.float32)
        rope_cos, rope_sin = precompute_rope(D_HEAD, MAX_SEQ_LEN)
        return {'x': x, 'wq': wq, 'wk': wk, 'wv': wv, 'wo': wo, 'q_norm_w': q_norm_w, 'k_norm_w': k_norm_w, 'rope_cos': rope_cos, 'rope_sin': rope_sin}
    _L1_attn_in = _L1_attn_setup()

    def _L1_ffn_setup():
        import jax, jax.numpy as jnp
        import numpy as np
        TOP_K = 4
        key = jax.random.key(seed)
        ks = jax.random.split(key, 9)
        B, T, D, H, NE = (2, 128, 256, 176, 16)
        s = 0.02
        return {'x': jax.random.normal(ks[0], (B, T, D), jnp.float32), 'gate_w': jax.random.normal(ks[1], (NE, D), jnp.float32) * s, 'gate_b': jax.random.normal(ks[2], (NE,), jnp.float32) * s, 'w1_shared': jax.random.normal(ks[3], (D, H), jnp.float32) * s, 'w2_shared': jax.random.normal(ks[4], (H, D), jnp.float32) * s, 'w3_shared': jax.random.normal(ks[5], (D, H), jnp.float32) * s, 'w1_routed': jax.random.normal(ks[6], (NE, D, H), jnp.float32) * s, 'w2_routed': jax.random.normal(ks[7], (NE, H, D), jnp.float32) * s, 'w3_routed': jax.random.normal(ks[8], (NE, D, H), jnp.float32) * s}
    _L1_ffn_in = _L1_ffn_setup()
    _d = {'L0_attn_x': _L0_attn_in['x'], 'L0_attn_W_qkv': _L0_attn_in['W_qkv'], 'L0_attn_W_o': _L0_attn_in['W_o'], 'L0_ffn_W1': _L0_ffn_in['W1'], 'L0_ffn_W2': _L0_ffn_in['W2'], 'L0_ffn_W3': _L0_ffn_in['W3'], 'L1_attn_wq': _L1_attn_in['wq'], 'L1_attn_wk': _L1_attn_in['wk'], 'L1_attn_wv': _L1_attn_in['wv'], 'L1_attn_wo': _L1_attn_in['wo'], 'L1_attn_q_norm_w': _L1_attn_in['q_norm_w'], 'L1_attn_k_norm_w': _L1_attn_in['k_norm_w'], 'L1_attn_rope_cos': _L1_attn_in['rope_cos'], 'L1_attn_rope_sin': _L1_attn_in['rope_sin'], 'L1_ffn_gate_w': _L1_ffn_in['gate_w'], 'L1_ffn_gate_b': _L1_ffn_in['gate_b'], 'L1_ffn_w1_shared': _L1_ffn_in['w1_shared'], 'L1_ffn_w2_shared': _L1_ffn_in['w2_shared'], 'L1_ffn_w3_shared': _L1_ffn_in['w3_shared'], 'L1_ffn_w1_routed': _L1_ffn_in['w1_routed'], 'L1_ffn_w2_routed': _L1_ffn_in['w2_routed'], 'L1_ffn_w3_routed': _L1_ffn_in['w3_routed']}
    _x0 = _d['L0_attn_x']
    _d['L0_attn_x'] = jax.random.normal(jax.random.fold_in(jax.random.key(seed), 1), (8, 256, 256), dtype=_x0.dtype)
    del _x0
    return _d

def reference(L0_attn_x, L0_attn_W_qkv, L0_attn_W_o, L0_ffn_W1, L0_ffn_W2, L0_ffn_W3, L1_attn_wq, L1_attn_wk, L1_attn_wv, L1_attn_wo, L1_attn_q_norm_w, L1_attn_k_norm_w, L1_attn_rope_cos, L1_attn_rope_sin, L1_ffn_gate_w, L1_ffn_gate_b, L1_ffn_w1_shared, L1_ffn_w2_shared, L1_ffn_w3_shared, L1_ffn_w1_routed, L1_ffn_w2_routed, L1_ffn_w3_routed):

    def _L0_attn_ref(x, W_qkv, W_o):
        import jax, jax.numpy as jnp
        import numpy as np
        import math
        N_EMBD = 256
        N_HEADS = 16
        HEAD_DIM = N_EMBD // N_HEADS
        CTX = 256

        def alibi_bias(seq_len: int, n_heads: int) -> jnp.ndarray:
            i = jnp.arange(seq_len)[:, None]
            j = jnp.arange(seq_len)[None, :]
            pos = jnp.where(j <= i, (j - i).astype(jnp.float32), 0.0)
            slopes = 2.0 ** (-8.0 / jnp.arange(1, n_heads + 1, dtype=jnp.float32))
            return slopes[:, None, None] * pos[None, :, :]

        def causal_mask(seq_len: int) -> jnp.ndarray:
            i = jnp.arange(seq_len)[:, None]
            j = jnp.arange(seq_len)[None, :]
            return jnp.where(j > i, -jnp.inf, 0.0).astype(jnp.float32)
        bsz, seq_len, n_embd = x.shape
        qkv = jnp.einsum('bsd,de->bse', x, W_qkv)
        q, k, v = jnp.split(qkv, 3, axis=-1)

        def to_heads(t):
            return t.reshape(bsz, seq_len, N_HEADS, HEAD_DIM).transpose(0, 2, 1, 3)
        q, k, v = (to_heads(q), to_heads(k), to_heads(v))
        attn = jnp.einsum('bhqd,bhkd->bhqk', q, k) / math.sqrt(HEAD_DIM)
        attn = attn + alibi_bias(seq_len, N_HEADS)[None] + causal_mask(seq_len)[None, None]
        attn = jax.nn.softmax(attn, axis=-1)
        y = jnp.einsum('bhqk,bhkd->bhqd', attn, v)
        y = y.transpose(0, 2, 1, 3).reshape(bsz, seq_len, n_embd)
        return jnp.einsum('bsd,de->bse', y, W_o)

    def _L0_ffn_ref(x, W1, W2, W3):
        import jax, jax.numpy as jnp
        import numpy as np
        B, S, D, H = (4, 256, 256, 1024)

        def fwht(x):
            orig_shape = x.shape
            n = orig_shape[-1]
            x = x.reshape(-1, n)
            h = 1
            while h < n:
                xb = x.reshape(-1, n // (2 * h), 2, h)
                a = xb[:, :, 0, :]
                b = xb[:, :, 1, :]
                x = jnp.stack([a + b, a - b], axis=2).reshape(-1, n)
                h *= 2
            scale = jnp.asarray(1.0 / np.sqrt(n), dtype=x.dtype)
            return (x * scale).reshape(orig_shape)
        up_gate = jnp.einsum('bsd,hd->bsh', x, W1)
        up_lin = jnp.einsum('bsd,hd->bsh', x, W3)
        hidden = jax.nn.silu(up_gate) * up_lin
        hidden = fwht(hidden)
        out = jnp.einsum('bsh,dh->bsd', hidden, W2)
        return out

    def _L1_attn_ref(x, wq, wk, wv, wo, q_norm_w, k_norm_w, rope_cos, rope_sin):
        import jax, jax.numpy as jnp
        import numpy as np
        B, T, D_MODEL = (2, 256, 256)
        N_HEADS, D_HEAD = (16, 128)
        MAX_SEQ_LEN = 256
        LOGIT_SOFTCAP = 50.0
        EPS = 1e-06

        def precompute_rope(dim, max_seq_len, theta=10000.0):
            freqs = 1.0 / theta ** (np.arange(0, dim, 2, dtype=np.float32) / dim)
            t = np.arange(max_seq_len, dtype=np.float32)
            angles = np.outer(t, freqs)
            return (jnp.asarray(np.cos(angles)), jnp.asarray(np.sin(angles)))

        def rmsnorm(x, w):
            return x * jax.lax.rsqrt(jnp.mean(x * x, axis=-1, keepdims=True) + EPS) * w

        def apply_rope(x, cos, sin):
            n = x.shape[1]
            x1, x2 = (x[..., ::2], x[..., 1::2])
            c = cos[:n][None, :, None, :]
            s = sin[:n][None, :, None, :]
            out = jnp.stack([x1 * c - x2 * s, x1 * s + x2 * c], axis=-1)
            return out.reshape(x.shape)
        Bx, Tx, _ = x.shape
        scale = D_HEAD ** (-0.5)
        q = (x @ wq.T).reshape(Bx, Tx, N_HEADS, D_HEAD).transpose(0, 2, 1, 3)
        k = (x @ wk.T).reshape(Bx, Tx, N_HEADS, D_HEAD).transpose(0, 2, 1, 3)
        v = (x @ wv.T).reshape(Bx, Tx, N_HEADS, D_HEAD).transpose(0, 2, 1, 3)
        q = rmsnorm(q, q_norm_w)
        k = rmsnorm(k, k_norm_w)
        q = apply_rope(q, rope_cos, rope_sin)
        k = apply_rope(k, rope_cos, rope_sin)
        scores = jnp.einsum('bhtd,bhsd->bhts', q, k) * scale
        scores = LOGIT_SOFTCAP * jnp.tanh(scores / LOGIT_SOFTCAP)
        mask = jnp.triu(jnp.ones((Tx, Tx), dtype=bool), k=1)
        scores = jnp.where(mask[None, None], -jnp.inf, scores)
        attn = jax.nn.softmax(scores, axis=-1)
        out = jnp.einsum('bhts,bhsd->bhtd', attn, v)
        out = out.transpose(0, 2, 1, 3).reshape(Bx, Tx, N_HEADS * D_HEAD)
        return out @ wo.T

    def _L1_ffn_ref(x, gate_w, gate_b, w1_shared, w2_shared, w3_shared, w1_routed, w2_routed, w3_routed):
        import jax, jax.numpy as jnp
        import numpy as np
        TOP_K = 4
        n_experts = w1_routed.shape[0]
        logits = jnp.einsum('ed,btd->bte', gate_w, x)
        scores = jax.nn.sigmoid(logits) + gate_b
        weights, indices = jax.lax.top_k(scores, TOP_K)
        weights = weights / weights.sum(-1, keepdims=True)
        shared_out = jax.nn.silu(x @ w1_shared) * (x @ w3_shared) @ w2_shared
        one_hot = jax.nn.one_hot(indices, n_experts, dtype=x.dtype)
        router_probs = (weights[..., None] * one_hot).sum(-2)
        h1 = jnp.einsum('btd,edc->btec', x, w1_routed)
        h2 = jnp.einsum('btd,edc->btec', x, w3_routed)
        h3 = jax.nn.silu(h1 * h2)
        experts_out = jnp.einsum('btec,ecd->bted', h3, w2_routed)
        routed_out = jnp.einsum('bted,bte->btd', experts_out, router_probs)
        return shared_out + routed_out
    x = L0_attn_x
    xn = _layernorm(x, axis=-1)
    s = _L0_attn_ref(xn, L0_attn_W_qkv, L0_attn_W_o)
    g = _silu(_L0_ffn_ref(xn, L0_ffn_W1, L0_ffn_W2, L0_ffn_W3))
    x = x + s * g
    xn = _layernorm(x, axis=-1)
    s = _L1_attn_ref(xn, L1_attn_wq, L1_attn_wk, L1_attn_wv, L1_attn_wo, L1_attn_q_norm_w, L1_attn_k_norm_w, L1_attn_rope_cos, L1_attn_rope_sin)
    g = _silu(_L1_ffn_ref(xn, L1_ffn_gate_w, L1_ffn_gate_b, L1_ffn_w1_shared, L1_ffn_w2_shared, L1_ffn_w3_shared, L1_ffn_w1_routed, L1_ffn_w2_routed, L1_ffn_w3_routed))
    x = x + s * g
    return x

_drawn_inputs = setup_inputs


def setup_inputs(seed=0):
    import zlib

    import numpy as np

    out = dict(_drawn_inputs(seed))
    spreads = {'L1_attn_q_norm_w': (1.0, 0.6), 'L1_attn_k_norm_w': (1.0, 0.6)}
    factors = {'L1_attn_wq': 8.0,
     'L1_attn_wk': 8.0,
     'L1_attn_wv': 8.0,
     'L1_attn_wo': 8.0,
     'L1_attn_rope_cos': 8.0,
     'L1_attn_rope_sin': 8.0,
     'L1_ffn_gate_w': 8.0,
     'L1_ffn_gate_b': 8.0,
     'L1_ffn_w1_shared': 8.0,
     'L1_ffn_w2_shared': 8.0,
     'L1_ffn_w3_shared': 8.0,
     'L1_ffn_w1_routed': 8.0,
     'L1_ffn_w2_routed': 8.0,
     'L1_ffn_w3_routed': 8.0}
    for name, (base, spread) in spreads.items():
        noise = np.random.default_rng([zlib.crc32(name.encode()), seed]).standard_normal(out[name].shape)
        drawn = base * np.exp(spread * noise) if base else spread * noise
        out[name] = jnp.asarray(drawn.astype(out[name].dtype))
    for name, factor in factors.items():
        out[name] = (out[name] * factor).astype(out[name].dtype)
    return out
```

```python
import concourse.bass as bass
from concourse import mybir
from contextlib import ExitStack

F32 = mybir.dt.float32
F32R = mybir.dt.float32r
BF16 = mybir.dt.bfloat16
ALU = mybir.AluOpType
ACT = mybir.ActivationFunctionType
AX = mybir.AxisListType

P = 128
NB, T, D = 8, 256, 256
TT, KD = T // P, D // P
NT = NB * TT
H0, E0 = 16, 16
HP = 32
NG = H0 * HP // P
GH = H0 // NG
FF = 1024
NJ = FF // P
H1, E1 = 16, 128
NU = H1 // 2
CAP = 50.0
NE, TOPK, HE = 16, 4, 176
NR = NE * HE // P
NC = NR + 2
NBLK, BLK = 4, 512
LN_EPS, RMS_EPS = 1e-5, 1e-6


def build(nc, x, pack_qk, pack_vo, pack_w1, pack_w3, pack_w2, pack_attn, pack_moe, gate_b, q_norm, k_norm,
          rope_cosT, rope_sinT, ident_c, hadamard_c, tri_add_c, tri_mul_c, alibi_q_c, alibi_k_c, expert_rows_c,
          before_c, out):
    ctx = ExitStack()
    with ctx:
        def sem(name):
            return ctx.enter_context(nc.semaphore(name))

        def sb(name, shape, dt=F32, stack=ctx):
            return stack.enter_context(nc.sbuf_tensor(name, shape, dt))

        banks = [ctx.enter_context(nc.psum_tensor(f"bank{i}", [P, 512], F32)) for i in range(2)]
        trio = ctx.enter_context(nc.psum_tensor("trio", [P, 3, 512], F32))
        more = ctx.enter_context(nc.psum_tensor("more", [P, 3, 512], F32))

        xs_all = sb("x_all", [P, NT, D])
        probT = sb("probT", [P, NB * T], F32R)
        ident = sb("ident", [P, P])
        raw = sb("raw", [P, 2, 2048])
        qk_scale = sb("qk_scale", [P, H1])
        tri_mul = sb("tri_mul", [P, P])
        half_pow = sb("half_pow", [P, 8])

        a_stack = ExitStack()

        def sa(name, shape, dt=F32):
            return sb(name, shape, dt, a_stack)

        wqk_h, wqk_l = sa("wqk_h", [P, 2, KD, 512], F32R), sa("wqk_l", [P, 2, KD, 512], F32R)
        wvo_h, wvo_l = sa("wvo_h", [P, 1280], F32R), sa("wvo_l", [P, 1280], F32R)
        w1_h, w1_l = sa("w1_h", [P, KD, FF], F32R), sa("w1_l", [P, KD, FF], F32R)
        w3_h, w3_l = sa("w3_h", [P, KD, FF], F32R), sa("w3_l", [P, KD, FF], F32R)
        w2_h, w2_l = sa("w2_h", [P, NJ, D], F32R), sa("w2_l", [P, NJ, D], F32R)
        hadamard, hadamard_r = sa("hadamard", [P, P]), sa("hadamard_r", [P, P], F32R)
        ident_b, tri_add = sa("ident_b", [P, P], BF16), sa("tri_add", [P, GH, P], BF16)
        tri_add32 = sa("tri_add32", [P, P])
        alibi_q, alibi_k = sa("alibi_q", [P, NG]), sa("alibi_k", [P, T])
        gate_bias, before = sa("gate_bias", [P, NE]), sa("before", [P, NE, NE])
        cosT_sb, sinT_sb, norm_w = sa("cosT_sb", [P, H1]), sa("sinT_sb", [P, H1]), sa("norm_w", [P, 2])
        st0, mv0, ve0, rs0 = sa("st0", [P, TT, 6]), sa("mv0", [P, TT, 2]), sa("ve0", [P, TT]), sa("rs0", [P, TT])
        waited = sa("waited", [P, 1])
        st1, mv1, ve1, rs1 = sa("st1", [P, TT, 6]), sa("mv1", [P, TT, 2]), sa("ve1", [P, TT]), sa("rs1", [P, TT])
        xn0, xn1 = sa("xn0", [P, TT, D]), sa("xn1", [P, TT, D])
        xT0h, xT0l = sa("xT0h", [P, KD, T], F32R), sa("xT0l", [P, KD, T], F32R)
        qT0, kT0 = sa("qT0", [P, 2, T]), sa("kT0", [P, NG, T])
        qz0 = sa("qz0", [P, NG, GH, T])
        v0 = sa("v0", [P, TT, H0, E0 + 1])
        nmax = sa("nmax", [P, NG, 2, GH])
        pex = sa("pex", [P, 3, GH, P])
        pT0 = sa("pT0", [P, 3, GH, P])
        rden0 = sa("rden0", [P, NG, TT, GH])
        y0 = sa("y0", [P, TT, D])
        yT0h, yT0l = sa("yT0h", [P, KD, T], F32R), sa("yT0l", [P, KD, T], F32R)
        s0 = sa("s0", [P, TT, D])
        th0, hid = sa("th0", [P, 2, T]), sa("hid", [P, 2, T])
        hid_h, hid_l = sa("hid_h", [P, 4, T], F32R), sa("hid_l", [P, 4, T], F32R)
        gate0 = sa("gate0", [P, TT, D])
        xT1h_c, xT1l_c = sa("xT1h_c", [P, KD, T], F32R), sa("xT1l_c", [P, KD, T], F32R)
        lgT = sa("lgT", [P, T])
        r_th, r_sc = sa("r_th", [P, TT, NE]), sa("r_sc", [P, TT, NE])
        r_gt, r_ge = sa("r_gt", [P, TT, NE, NE]), sa("r_ge", [P, TT, NE, NE])
        r_rank, r_w = sa("r_rank", [P, TT, NE]), sa("r_w", [P, TT, NE])
        r_sum, r_p = sa("r_sum", [P, TT]), sa("r_p", [P, TT, NE])
        r_split = sa("r_split", [P, TT, P], F32R)
        a_stack.close()

        b_stack = ExitStack()

        def sbb(name, shape, dt=F32):
            return sb(name, shape, dt, b_stack)

        xT1h = sb("xT1h", [P, KD, NB * T], F32R)
        xT1l = sb("xT1l", [P, KD, NB * T], F32R)
        s_acc = sb("s_acc", [P, NT, D])
        expert_rows = sb("expert_rows", [P, NR * P])
        bw_h, bw_l = sbb("bw_h", [P, 2, 2048], F32R), sbb("bw_l", [P, 2, 2048], F32R)
        xs = sbb("xs", [P, 2, TT, 2, 2, E1])
        sq = sbb("sq", [P, TT, 512])
        qn = sbb("qn", [P, 2, TT, 2, E1])
        ssq, msq, rstd = sbb("ssq", [P, 2, TT, 4]), sbb("msq", [P, 2, 8]), sbb("rstd", [P, 2, 8])
        v1 = sbb("v1", [P, 4, TT, 2, E1 + 1])
        qT1, kT1 = sbb("qT1", [P, 2, 2, T]), sbb("kT1", [P, 2, 2, T])
        pT1 = sbb("pT1", [P, 2, 2, 3 * P])
        rden1 = sbb("rden1", [P, 2, TT, 2])
        y1 = sbb("y1", [P, 2, TT, 2, E1])
        yT1h, yT1l = sbb("yT1h", [P, 2, 2, T], F32R), sbb("yT1l", [P, 2, 2, T], F32R)
        b_stack.close()

        rows_cur = sb("rows_cur", [P, 2, 2, P], F32R)
        acc = sb("acc", [P, KD, NB * T])
        cw_h, cw_l = sb("cw_h", [P, 2, 1536], F32R), sb("cw_l", [P, 2, 1536], F32R)
        h3, u, th1 = sb("h3", [P, 2, BLK]), sb("u", [P, 2, BLK]), sb("th1", [P, 2, BLK])
        w_u, z1 = sb("w_u", [P, 2, BLK]), sb("z1", [P, 2, BLK])
        z1h, z1l = sb("z1h", [P, 2, BLK], F32R), sb("z1l", [P, 2, BLK], F32R)
        th_o, g_o = sb("th_o", [P, KD, BLK]), sb("g_o", [P, KD, BLK])
        xT1_dram = nc.dram_tensor("xT1_scratch", [2, NB, P, KD * T], F32).ap()

        x0_loaded, x_loaded, consts_loaded = sem("x0_loaded"), sem("x_loaded"), sem("consts_loaded")
        raw_loaded = [sem("raw_loaded0"), sem("raw_loaded1")]
        expert_loaded, out_stored = sem("expert_loaded"), sem("out_stored")
        consts_made, rope_made, pow_made = sem("consts_made"), sem("rope_made"), sem("pow_made")
        wa_hi, wa_lo_v, wa_lo_p = sem("wa_hi"), sem("wa_lo_v"), sem("wa_lo_p")
        fw_step, fw_hi, fw_lo, fw_done, w2_hi, w2_lo = (sem(n) for n in (
            "fw_step", "fw_hi", "fw_lo", "fw_done", "w2_hi", "w2_lo"))
        xT0_ps, qk0_ps, v0_ps, s0_ps, pT0_ps, y0_ps, yT0_ps, o0_ps, up_ps, down_ps = (sem(n) for n in (
            "xT0_ps", "qk0_ps", "v0_ps", "s0_ps", "pT0_ps", "y0_ps", "yT0_ps", "o0_ps", "up_ps", "down_ps"))
        xT1_ps, lgT_ps, lg_ps, probT_ps = (sem(n) for n in ("xT1_ps", "lgT_ps", "lg_ps", "probT_ps"))
        xT0h_sb, v0_sb, exp0, pT0_sb, yT0h_sb, s0_sb, th0_sb, hidh_sb = (sem(n) for n in (
            "xT0h_sb", "v0_sb", "exp0", "pT0_sb", "yT0h_sb", "s0_sb", "th0_sb", "hidh_sb"))
        thf_sb, xT1h_sb, lgT_sb, rth_sb, probT_sb = (sem(n) for n in (
            "thf_sb", "xT1h_sb", "lgT_sb", "rth_sb", "probT_sb"))
        qT0_sb, qz0_sb, qz0_zero, xT1_stored = (sem(n) for n in (
            "qT0_sb", "qz0_sb", "qz0_zero", "xT1_stored"))
        xT1_loaded = [sem(f"xT1_loaded{b}") for b in range(NB)]
        st0_sb, mv0_sb, ve0_sb, rs0_sb, xn0_sb = (sem(n) for n in ("st0_sb", "mv0_sb", "ve0_sb", "rs0_sb", "xn0_sb"))
        st1_sb, mv1_sb, ve1_sb, rs1_sb, xn1_sb = (sem(n) for n in ("st1_sb", "mv1_sb", "ve1_sb", "rs1_sb", "xn1_sb"))
        xT0l_sb, xT1l_sb, qk0_sb, max0, z0_sb, hid_sb, hidl_sb = (sem(n) for n in (
            "xT0l_sb", "xT1l_sb", "qk0_sb", "max0", "z0_sb", "hid_sb", "hidl_sb"))
        rden0_sb, y0_sb, yT0l_sb, gf_sb, sgf_sb, x1_sb, route, split_sb = (sem(n) for n in (
            "rden0_sb", "y0_sb", "yT0l_sb", "gf_sb", "sgf_sb", "x1_sb", "route", "split_sb"))
        split_hi = sem("split_hi")
        qk1_ps, v1_ps, qT1_ps, kT1_ps, s1_ps, y1_ps, yT1_ps, o1_ps = (sem(n) for n in (
            "qk1_ps", "v1_ps", "qT1_ps", "kT1_ps", "s1_ps", "y1_ps", "yT1_ps", "o1_ps"))
        xs_sb, sq_sb, v1_sb, qT1_sb, tanh1, exp1, yT1h_sb, bw_hi = (sem(n) for n in (
            "xs_sb", "sq_sb", "v1_sb", "qT1_sb", "tanh1", "exp1", "yT1h_sb", "bw_hi"))
        ssq_sb, msq_sb, rstd_sb, qn_sb, masked1 = (sem(n) for n in ("ssq_sb", "msq_sb", "rstd_sb", "qn_sb", "masked1"))
        kT1_sb, rden1_sb, y1_sb, yT1l_sb, acc1, bw_lo, v1_ones = (sem(n) for n in (
            "kT1_sb", "rden1_sb", "y1_sb", "yT1l_sb", "acc1", "bw_lo", "v1_ones"))
        up1_ps, gate_ps, prob_ps, down1_ps, gT_ps = (sem(n) for n in ("up1_ps", "gate_ps", "prob_ps", "down1_ps", "gT_ps"))
        h3_sb, u_sb, th1_sb, wu_sb, z1_sb, z1h_sb, z1l_sb, acc_sb = (sem(n) for n in (
            "h3_sb", "u_sb", "th1_sb", "wu_sb", "z1_sb", "z1h_sb", "z1l_sb", "acc_sb"))
        cw_hi, cw_lo, rows_made, tho_sb, go_sb, so_sb, o_sb_made = (sem(n) for n in (
            "cw_hi", "cw_lo", "rows_made", "tho_sb", "go_sb", "so_sb", "o_sb_made"))

        N_CONST = 12

        def after(eng, s, value):
            if isinstance(value, int) and value <= 0:
                return
            eng.wait_ge(s, value)

        A_LOADS, C_PAIRS = 5, NC // 2

        def raw_ready(eng, n):
            eng.wait_ge(raw_loaded[n % 2], 16 * (n // 2 + 1))

        block = ctx.enter_context(nc.Block())

        @block.sync
        def _(sp):
            sp.dma_start(xs_all[:, 0:TT, :], x[0].rearrange("(t p) d -> p t d", p=P)).then_inc(x0_loaded, 16)
            sp.dma_start(raw[:, 0, :], pack_qk).then_inc(raw_loaded[0], 16)
            sp.dma_start(raw[:, 1, 0:1280], pack_vo).then_inc(raw_loaded[1], 16)
            for dst, src in ((ident, ident_c), (alibi_q, alibi_q_c), (alibi_k, alibi_k_c), (tri_add32, tri_add_c),
                             (hadamard, hadamard_c), (tri_mul, tri_mul_c), (before, before_c)):
                sp.dma_start(dst[:], src).then_inc(consts_loaded, 16)
            sp.dma_start(gate_bias[:], gate_b.partition_broadcast(P)).then_inc(consts_loaded, 16)
            sp.dma_start(norm_w[:, 0:1], q_norm).then_inc(consts_loaded, 16)
            sp.dma_start(norm_w[:, 1:2], k_norm).then_inc(consts_loaded, 16)
            sp.dma_start(cosT_sb[:], rope_cosT).then_inc(consts_loaded, 16)
            sp.dma_start(sinT_sb[:], rope_sinT).then_inc(consts_loaded, 16)
            sp.dma_start(xs_all[:, TT:NT, :],
                         x[1:NB].rearrange("b (t p) d -> p (b t) d", p=P)).then_inc(x_loaded, 16)
            sp.wait_ge(wa_hi, 1)
            sp.wait_ge(wa_lo_v, 1)
            sp.dma_start(raw[:, 0, :], pack_w1).then_inc(raw_loaded[0], 16)
            sp.wait_ge(wa_hi, 2)
            sp.wait_ge(wa_lo_v, 2)
            sp.dma_start(raw[:, 1, :], pack_w3).then_inc(raw_loaded[1], 16)
            sp.wait_ge(wa_hi, 3)
            sp.wait_ge(wa_lo_p, 1)
            sp.dma_start(raw[:, 0, :], pack_w2).then_inc(raw_loaded[0], 16)
            sp.wait_ge(fw_lo, 1)
            for n in range(2):
                sp.dma_start(raw[:, (A_LOADS + n) % 2, :], pack_attn[n]).then_inc(raw_loaded[(A_LOADS + n) % 2], 16)
            with sp.Fori(0, NB) as b:
                sp.wait_ge(xT1l_sb, b + 1)
                for s, part in enumerate((xT1h_c, xT1l_c)):
                    sp.dma_start(xT1_dram[s, bass.ds(b, 1)].rearrange("a p n -> p (a n)"),
                                 part[:].bitcast(F32).rearrange("p k t -> p (k t)")).then_inc(xT1_stored, 16)
            sp.wait_ge(xT1_stored, 32 * NB)
            sp.wait_ge(probT_sb, NB)
            for b in range(NB):
                for s, part in enumerate((xT1h, xT1l)):
                    sp.dma_start(part[:, :, b * T:(b + 1) * T].bitcast(F32),
                                 xT1_dram[s, b].rearrange("p (k t) -> p k t", k=KD)).then_inc(xT1_loaded[b], 16)
            sp.dma_start(expert_rows[:], expert_rows_c).then_inc(expert_loaded, 16)
            with sp.Fori(0, NU // 2 - 1) as w:
                for n in range(2):
                    sp.wait_ge(bw_hi, 4 * (2 * w + n + 1))
                    sp.wait_ge(bw_lo, 4 * (2 * w + n + 1))
                    half = (A_LOADS + n) % 2
                    sp.dma_start(raw[:, half, :], pack_attn[bass.ds(2 * w + n + 2, 1)].rearrange("a p n -> p (a n)"))\
                      .then_inc(raw_loaded[half], 16)
            for n in range(2):
                sp.wait_ge(bw_hi, 4 * (NU - 1 + n))
                sp.wait_ge(bw_lo, 4 * (NU - 1 + n))
                half = (A_LOADS + NU + n) % 2
                sp.dma_start(raw[:, half, 0:1536], pack_moe[n]).then_inc(raw_loaded[half], 16)
            with sp.Fori(0, C_PAIRS // 2 - 1) as w:
                for n in range(2):
                    sp.wait_ge(cw_hi, 3 * (2 * w + n + 1))
                    sp.wait_ge(cw_lo, 3 * (2 * w + n + 1))
                    half = (A_LOADS + NU + n) % 2
                    sp.dma_start(raw[:, half, 0:1536],
                                 pack_moe[bass.ds(2 * w + n + 2, 1)].rearrange("a p n -> p (a n)"))\
                      .then_inc(raw_loaded[half], 16)
            for n in range(NT // 2):
                sp.wait_ge(o_sb_made, n + 1)
                sp.dma_start(out[n].rearrange("(t p) d -> p t d", p=P), xs_all[:, 2 * n:2 * n + 2, :])\
                  .then_inc(out_stored, 16)
            sp.wait_ge(out_stored, 16 * (NT // 2))

        @block.tensor
        def _(pe):
            def bank(n):
                return banks[n % 2]

            def three(o, wh, wl, mh, ml, first, last):
                pe.matmul(o, wh, mh, start=first, stop=False)
                pe.matmul(o, wl, mh, start=False, stop=False)
                return pe.matmul(o, wh, ml, start=False, stop=last)

            def norm_T0(b):
                pe.wait_ge(xn0_sb, 2 * b + 2)
                o = bank(20)[:, :].rearrange("p (k t) -> p k t", k=KD)
                for t in range(TT):
                    for k in range(KD):
                        last = pe.transpose(o[:, k, t * P:(t + 1) * P], xn0[:, t, k * P:(k + 1) * P], ident[:])
                last.then_inc(xT0_ps, 1)

            def up(b, j):
                n = {0: 5, 1: 6, 2: 8, 3: 9, 4: 11, 5: 13, 6: 16, 7: 19}[j]
                o = bank(n)[:, :].rearrange("p (g t) -> p g t", g=2)
                for g, (wh, wl) in enumerate(((w1_h, w1_l), (w3_h, w3_l))):
                    for k in range(KD):
                        last = three(o[:, g, :], wh[:, k, j * P:(j + 1) * P], wl[:, k, j * P:(j + 1) * P],
                                     xT0h[:, k, :], xT0l[:, k, :], k == 0, k == KD - 1)
                last.then_inc(up_ps, 1)

            def scores(b, g):
                pe.wait_ge(qz0_sb, 4 * b + g + 1)
                pe.wait_ge(qk0_sb, 4 * b + g + 1)
                after(pe, exp0, 4 * b + g)
                for t in range(TT):
                    pe.matmul(trio[:, 2 * t, :], ident_b[:], tri_add[:].rearrange("p h k -> p (h k)"),
                              start=True, stop=False, skip_group_check=True)
                    for h in range(GH):
                        last = pe.matmul(trio[:, 2 * t, h * P:(h + 1) * P], qz0[:, g, h, t * P:(t + 1) * P],
                                         kT0[:, g, t * P:(t + 1) * P], start=False, stop=h == GH - 1,
                                         skip_group_check=True)
                for h in range(GH):
                    last = pe.matmul(trio[:, 1, h * P:(h + 1) * P], qz0[:, g, h, P:T], kT0[:, g, 0:P],
                                     start=True, stop=True)
                last.then_inc(s0_ps, 1)

            def probs_T(b, g):
                pe.wait_ge(exp0, 4 * b + g + 1)
                for i in range(3):
                    n = 3 * g + i
                    after(pe, pT0_sb, 12 * b + n - 1)
                    o = more[:, n % 2, :].rearrange("p (h q) -> p h q", h=GH)
                    for h in range(GH):
                        last = pe.transpose(o[:, h, :], pex[:, i, h, :], ident[:])
                    last.then_inc(pT0_ps, 1)

            def mix(b, g):
                n = {0: 10, 1: 14, 2: 17, 3: 21}[g]
                pe.wait_ge(pT0_sb, 12 * b + 3 * g + 3)
                if g == 0:
                    pe.wait_ge(v0_sb, b + 1)
                o = bank(n)[:, 0:TT * GH * (E0 + 1)].rearrange("p (t h e) -> p t h e", t=TT, h=GH)
                for h in range(GH):
                    hh = g * GH + h
                    pe.matmul(o[:, 0, h, :], pT0[:, 0, h, :], v0[:, 0, hh, :], start=True, stop=True)
                    pe.matmul(o[:, 1, h, :], pT0[:, 1, h, :], v0[:, 0, hh, :], start=True, stop=False)
                    last = pe.matmul(o[:, 1, h, :], pT0[:, 2, h, :], v0[:, 1, hh, :], start=False, stop=True)
                last.then_inc(y0_ps, 1)

            def down(b, j):
                pe.wait_ge(hidl_sb, 8 * b + j + 1)
                o = more[:, 2, :].rearrange("p (t d) -> p t d", t=TT)
                for t in range(TT):
                    c = slice(t * P, (t + 1) * P)
                    pe.matmul(o[:, t, :], hid_h[:, j % 4, c], w2_h[:, j, :], start=(j == 0 and t == 0), stop=False,
                              skip_group_check=True)
                    pe.matmul(o[:, t, :], hid_l[:, j % 4, c], w2_h[:, j, :], start=False, stop=False, skip_group_check=True)
                    last = pe.matmul(o[:, t, :], hid_h[:, j % 4, c], w2_l[:, j, :], start=False, stop=j == NJ - 1,
                                     skip_group_check=True)
                last.then_inc(down_ps, 1)

            def norm_T1(b):
                pe.wait_ge(xn1_sb, 2 * b + 2)
                o = bank(7)[:, :].rearrange("p (k t) -> p k t", k=KD)
                for t in range(TT):
                    for k in range(KD):
                        last = pe.transpose(o[:, k, t * P:(t + 1) * P], xn1[:, t, k * P:(k + 1) * P], ident[:])
                last.then_inc(xT1_ps, 1)

            def logits_T(b):
                pe.wait_ge(xT1l_sb, b + 1)
                gate = [w[:, 1024:1280].rearrange("p (k e) -> p k e", k=KD) for w in (wvo_h, wvo_l)]
                for k in range(KD):
                    last = three(bank(12)[:, 0:T], gate[0][:, k, :], gate[1][:, k, :], xT1h_c[:, k, :], xT1l_c[:, k, :],
                                 k == 0, k == KD - 1)
                last.then_inc(lgT_ps, 1)

            def logits(b):
                pe.wait_ge(lgT_sb, b + 1)
                for t in range(TT):
                    last = pe.transpose(bank(15)[:, t * P:(t + 1) * P], lgT[:, t * P:(t + 1) * P], ident[:])
                last.then_inc(lg_ps, 1)

            def route_T(b):
                pe.wait_ge(split_sb, b + 1)
                for t in range(TT):
                    last = pe.transpose(bank(18)[:, t * P:(t + 1) * P], r_split[:, t, :].bitcast(F32), ident[:])
                last.then_inc(probT_ps, 1)

            def batch(b, first, final):
                t = b - 1
                pe.wait_ge(xT0l_sb, b + 1)
                if first:
                    pe.wait_ge(wa_lo_v, 1)
                for g in range(NG):
                    if g == 0:
                        after(pe, yT0l_sb, b)
                    elif g == 1:
                        after(pe, s0_sb, b)
                    else:
                        pe.wait_ge(qk0_sb, 4 * b + g - 1)
                    o = bank(g)[:, :].rearrange("p (s t) -> p s t", s=2)
                    for s in range(2):
                        for k in range(KD):
                            c = slice(g * P, (g + 1) * P)
                            last = three(o[:, s, :], wqk_h[:, s, k, c], wqk_l[:, s, k, c], xT0h[:, k, :], xT0l[:, k, :],
                                         k == 0, k == KD - 1)
                    last.then_inc(qk0_ps, 1)
                pe.wait_ge(qk0_sb, 4 * b + 3)
                if first:
                    pe.wait_ge(wa_lo_v, 2)
                o = bank(4)[:, :].rearrange("p (t d) -> p t d", t=TT)
                wv = [w[:, 0:512].rearrange("p (k d) -> p k d", k=KD) for w in (wvo_h, wvo_l)]
                for tt in range(TT):
                    for k in range(KD):
                        c = slice(tt * P, (tt + 1) * P)
                        pe.matmul(o[:, tt, :], xT0h[:, k, c], wv[0][:, k, :], start=k == 0, stop=False)
                        pe.matmul(o[:, tt, :], xT0l[:, k, c], wv[0][:, k, :], start=False, stop=False)
                        last = pe.matmul(o[:, tt, :], xT0h[:, k, c], wv[1][:, k, :], start=False, stop=k == KD - 1)
                last.then_inc(v0_ps, 1)
                scores(b, 0)
                if first:
                    pe.wait_ge(wa_lo_p, 2)
                pe.wait_ge(qk0_sb, 4 * b + 4)
                up(b, 0)
                pe.wait_ge(v0_sb, b + 1)
                up(b, 1)
                if not first:
                    pe.wait_ge(hid_sb, 8 * b + 1)
                    norm_T1(t)
                pe.wait_ge(hid_sb, 8 * b + 2)
                up(b, 2)
                scores(b, 1)
                probs_T(b, 0)
                after(pe, xT1l_sb, b)
                if first:
                    pe.wait_ge(hid_sb, 8 * b + 1)
                up(b, 3)
                pe.wait_ge(hid_sb, 8 * b + 3)
                mix(b, 0)
                if first:
                    pe.wait_ge(fw_lo, 1)
                    pe.wait_ge(y0_sb, 1)
                    pe.wait_ge(hid_sb, 4)
                    for i in range(4):
                        if i >= 2:
                            pe.wait_ge(w2_lo, i - 1)
                        c = slice(2 * i, 2 * i + 2)
                        o = bank(i)[:, :].rearrange("p (j d) -> p j d", j=2)
                        pe.matmul(o, hadamard_r[:], w2_h[:, c, :], start=True, stop=False)
                        pe.matmul(o, hadamard_r[:], w2_l[:, c, :], start=False, stop=True).then_inc(fw_done, 1)
                    pe.wait_ge(w2_lo, 4)
                after(pe, gf_sb, b)
                down(b, 0)
                down(b, 1)
                pe.wait_ge(hid_sb, 8 * b + 4)
                up(b, 4)
                if not first:
                    pe.wait_ge(y0_sb, 4 * b + 1)
                    logits_T(t)
                scores(b, 2)
                probs_T(b, 1)
                pe.wait_ge(hid_sb, 8 * b + 5)
                up(b, 5)
                pe.wait_ge(y0_sb, 4 * b + 1)
                after(pe, lgT_sb, b)
                mix(b, 1)
                down(b, 2)
                down(b, 3)
                pe.wait_ge(hid_sb, 8 * b + 6)
                if not first:
                    logits(t)
                scores(b, 3)
                probs_T(b, 2)
                pe.wait_ge(y0_sb, 4 * b + 2)
                up(b, 6)
                after(pe, rth_sb, b)
                mix(b, 2)
                down(b, 4)
                down(b, 5)
                pe.wait_ge(hid_sb, 8 * b + 7)
                if not first:
                    route_T(t)
                pe.wait_ge(y0_sb, 4 * b + 3)
                up(b, 7)
                after(pe, probT_sb, b)
                if not final:
                    norm_T0(b + 1)
                probs_T(b, 3)
                pe.wait_ge(hid_sb, 8 * b + 8)
                mix(b, 3)
                down(b, 6)
                if not final:
                    pe.wait_ge(xT0l_sb, b + 2)
                pe.wait_ge(y0_sb, 4 * b + 4)
                o = bank(22)[:, :].rearrange("p (k t) -> p k t", k=KD)
                for tt in range(TT):
                    for k in range(KD):
                        last = pe.transpose(o[:, k, tt * P:(tt + 1) * P], y0[:, tt, k * P:(k + 1) * P], ident[:])
                last.then_inc(yT0_ps, 1)
                down(b, 7)
                pe.wait_ge(yT0l_sb, b + 1)
                o = bank(23)[:, :].rearrange("p (t d) -> p t d", t=TT)
                wo = [w[:, 512:1024].rearrange("p (k d) -> p k d", k=KD) for w in (wvo_h, wvo_l)]
                for tt in range(TT):
                    for k in range(KD):
                        c = slice(tt * P, (tt + 1) * P)
                        pe.matmul(o[:, tt, :], yT0h[:, k, c], wo[0][:, k, :], start=k == 0, stop=False)
                        pe.matmul(o[:, tt, :], yT0l[:, k, c], wo[0][:, k, :], start=False, stop=False)
                        last = pe.matmul(o[:, tt, :], yT0h[:, k, c], wo[1][:, k, :], start=False, stop=k == KD - 1)
                last.then_inc(o0_ps, 1)

            pe.wait_ge(consts_loaded, 16 * N_CONST)
            norm_T0(0)
            pe.wait_ge(consts_made, 1)
            batch(0, True, False)
            with pe.Fori(1, NB - 1) as b:
                batch(b, False, False)
            batch(NB - 1, False, True)
            t = NB - 1
            pe.wait_ge(s0_sb, NB)
            norm_T1(t)
            pe.wait_ge(yT0l_sb, NB)
            logits_T(t)
            pe.wait_ge(xT1l_sb, NB)
            logits(t)
            pe.wait_ge(lgT_sb, NB)
            route_T(t)

            tr = [trio[:, 2, :], more[:, 2, :]]
            s_b = trio[:, 0:2, :]
            y_b = more[:, 0:2, :]

            def project_qk(n, i, tt):
                b, par = i % NB, (i // NB) % 2
                w = [v[:, par, 0:1024].rearrange("p (k c) -> p k c", k=KD) for v in (bw_h, bw_l)]
                c = slice(b * T + tt * P, b * T + (tt + 1) * P)
                for k in range(KD):
                    pe.matmul(banks[tt][:, :], xT1h[:, k, c], w[0][:, k, :], start=k == 0, stop=False)
                    pe.matmul(banks[tt][:, :], xT1l[:, k, c], w[0][:, k, :], start=False, stop=False)
                    last = pe.matmul(banks[tt][:, :], xT1h[:, k, c], w[1][:, k, :], start=False, stop=k == KD - 1)
                last.then_inc(qk1_ps, 1)

            def project_v(n, i):
                b, par = i % NB, (i // NB) % 2
                w = [v[:, par, 1024:1536].rearrange("p (k c) -> p k c", k=KD) for v in (bw_h, bw_l)]
                o = banks[0][:, :].rearrange("p (t c) -> p t c", t=TT)
                for tt in range(TT):
                    c = slice(b * T + tt * P, b * T + (tt + 1) * P)
                    for k in range(KD):
                        pe.matmul(o[:, tt, :], xT1h[:, k, c], w[0][:, k, :], start=k == 0, stop=False)
                        pe.matmul(o[:, tt, :], xT1l[:, k, c], w[0][:, k, :], start=False, stop=False)
                        last = pe.matmul(o[:, tt, :], xT1h[:, k, c], w[1][:, k, :], start=False, stop=k == KD - 1)
                last.then_inc(v1_ps, 1)

            def transposes_qk(n, i):
                r = i % 2
                pe.wait_ge(xs_sb, 2 * n + 2)
                o = tr[1].rearrange("p (h t) -> p h t", h=2)
                for tt in range(TT):
                    for h in range(2):
                        last = pe.transpose(o[:, h, tt * P:(tt + 1) * P], xs[:, r, tt, 1, h, :], ident[:])
                last.then_inc(kT1_ps, 1)
                pe.wait_ge(qn_sb, n + 1)
                o = tr[0].rearrange("p (h t) -> p h t", h=2)
                for tt in range(TT):
                    for h in range(2):
                        last = pe.transpose(o[:, h, tt * P:(tt + 1) * P], qn[:, r, tt, h, :], ident[:])
                last.then_inc(qT1_ps, 1)

            def scores1(n, i):
                r = i % 2
                pe.wait_ge(qT1_sb, n + 1)
                pe.wait_ge(kT1_sb, n + 1)
                after(pe, tanh1, n)
                for h in range(2):
                    pe.matmul(s_b[:, 0, h * T:(h + 1) * T], kT1[:, r, h, 0:P], qT1[:, r, h, :], start=True, stop=True)
                    last = pe.matmul(s_b[:, 1, h * P:(h + 1) * P], kT1[:, r, h, P:T], qT1[:, r, h, P:T],
                                     start=True, stop=True)
                last.then_inc(s1_ps, 1)

            def mix1(n, i):
                r = i % 2
                pe.wait_ge(masked1, n + 1)
                pe.wait_ge(v1_sb, n + 1)
                after(pe, y1_sb, n)
                w = E1 + 1
                for h in range(2):
                    p = pT1[:, r, h, :]
                    o = [y_b[:, tt, h * w:(h + 1) * w] for tt in range(TT)]
                    pe.matmul(o[0], p[:, 0:P], v1[:, i % 4, 0, h, :], start=True, stop=True)
                    pe.matmul(o[1], p[:, P:T], v1[:, i % 4, 0, h, :], start=True, stop=False)
                    last = pe.matmul(o[1], p[:, T:T + P], v1[:, i % 4, 1, h, :], start=False, stop=True)
                last.then_inc(y1_ps, 1)

            def transposes_y(n, i):
                pe.wait_ge(y1_sb, n + 1)
                o = tr[0].rearrange("p (h t) -> p h t", h=2)
                for tt in range(TT):
                    for h in range(2):
                        last = pe.transpose(o[:, h, tt * P:(tt + 1) * P], y1[:, i % 2, tt, h, :], ident[:])
                last.then_inc(yT1_ps, 1)

            def project_o(n, i):
                par, r = (i // NB) % 2, i % 2
                pe.wait_ge(yT1l_sb, n + 1)
                w = [v[:, par, 1536:2048].rearrange("p (h d) -> p h d", h=2) for v in (bw_h, bw_l)]
                o = banks[1][:, :].rearrange("p (t d) -> p t d", t=TT)
                for tt in range(TT):
                    c = slice(tt * P, (tt + 1) * P)
                    for h in range(2):
                        pe.matmul(o[:, tt, :], yT1h[:, r, h, c], w[0][:, h, :], start=h == 0, stop=False)
                        pe.matmul(o[:, tt, :], yT1l[:, r, h, c], w[0][:, h, :], start=False, stop=False)
                        last = pe.matmul(o[:, tt, :], yT1h[:, r, h, c], w[1][:, h, :], start=False, stop=h == 1)
                last.then_inc(o1_ps, 1)

            def unit_pair(w, first):
                for i in range(2 * NB):
                    n = 2 * NB * w + i
                    if i % NB == 0:
                        pe.wait_ge(bw_lo, 4 * (2 * w + i // NB + 1))
                    after(pe, v1_sb, n)
                    if first and i == 0:
                        pe.wait_ge(probT_sb, NB)
                    if first and i < NB:
                        pe.wait_ge(xT1_loaded[i], 32)
                    project_qk(n, i, 0)
                    after(pe, acc1, n - 3)
                    if first and i == 0:
                        pe.wait_ge(rth_sb, NB)
                    project_qk(n, i, 1)
                    pe.wait_ge(sq_sb, 2 * n + 1)
                    project_v(n, i)
                    if not first or i >= 1:
                        if not first or i >= 3:
                            pe.wait_ge(yT1l_sb, n - 2)
                        transposes_qk(n - 1, i - 1)
                    if not first or i >= 2:
                        mix1(n - 2, i - 2)
                    pe.wait_ge(sq_sb, 2 * n + 2)
                    if not first or i >= 3:
                        project_o(n - 3, i - 3)
                    if not first or i >= 1:
                        scores1(n - 1, i - 1)
                    if not first or i >= 2:
                        pe.wait_ge(qT1_sb, n)
                        transposes_y(n - 2, i - 2)

            unit_pair(0, True)
            with pe.Fori(1, NU // 2) as w:
                unit_pair(w, False)
            n = NU * NB
            pe.wait_ge(yT1l_sb, n - 2)
            transposes_qk(n - 1, -1)
            mix1(n - 2, -2)
            pe.wait_ge(acc1, n - 3)
            project_o(n - 3, -3)
            scores1(n - 1, -1)
            pe.wait_ge(qT1_sb, n)
            transposes_y(n - 2, -2)
            pe.wait_ge(acc1, n - 2)
            project_o(n - 2, -2)
            mix1(n - 1, -1)
            pe.wait_ge(yT1l_sb, n - 1)
            transposes_y(n - 1, -1)
            pe.wait_ge(acc1, n - 1)
            project_o(n - 1, -1)

            b1 = [banks[0][:, :], banks[1][:, :]]
            b3 = [trio[:, 0, :], trio[:, 1, :]]
            bp = [trio[:, 2, :], more[:, 0, :]]
            bo = [more[:, 1, :], more[:, 2, :]]

            def hidden_up(m, i):
                par, blk, c, r = (i // 8) % 2, (i % 8) // 2, i % 2, i % 2
                cols = slice(blk * BLK, (blk + 1) * BLK)
                for s, o, read, done in ((0, b1[r], u_sb, up1_ps), (1, b3[r], h3_sb, gate_ps)):
                    w = [v[:, par, 512 * s:512 * s + 512].rearrange("p (k c h) -> p k c h", k=KD, c=2)
                         for v in (cw_h, cw_l)]
                    after(pe, read, m - 1)
                    for k in range(KD):
                        last = three(o, w[0][:, k, c, :], w[1][:, k, c, :], xT1h[:, k, cols], xT1l[:, k, cols],
                                     k == 0, k == KD - 1)
                    last.then_inc(done, 1)

            def spread_probs(m, i):
                par, blk, c, r = (i // 8) % 2, (i % 8) // 2, i % 2, i % 2
                after(pe, wu_sb, m - 1)
                pe.matmul(bp[r], rows_cur[:, par, c, :], probT[:, blk * BLK:(blk + 1) * BLK],
                          start=True, stop=True).then_inc(prob_ps, 1)

            def hidden_down(m, i):
                par, c, r = (i // 8) % 2, i % 2, i % 2
                pe.wait_ge(z1l_sb, m + 1)
                w = [v[:, par, 1024:1536].rearrange("p (c d) -> p c d", c=2) for v in (cw_h, cw_l)]
                if c == 0:
                    after(pe, acc_sb, m)
                for k in range(KD):
                    d = slice(k * P, (k + 1) * P)
                    last = three(bo[k], w[0][:, c, d], w[1][:, c, d], z1h[:, r, :], z1l[:, r, :], c == 0, c == 1)
                last.then_inc(down1_ps, 1)

            def four_chunks(w, first, final):
                for i in range(16):
                    m = 16 * w + i
                    shared = final and i >= 8
                    if i % 8 == 0:
                        pe.wait_ge(cw_lo, 3 * (2 * w + i // 8 + 1))
                        if not shared:
                            pe.wait_ge(rows_made, 2 * w + i // 8 + 1)
                    hidden_up(m, i)
                    if not shared:
                        spread_probs(m, i)
                    if not first or i >= 2:
                        hidden_down(m - 2, i - 2)

            pe.wait_ge(acc1, NU * NB)
            four_chunks(0, True, False)
            with pe.Fori(1, NC // 4 - 1) as w:
                four_chunks(w, False, False)
            four_chunks(NC // 4 - 1, False, True)
            m = 16 * (NC // 4)
            hidden_down(m - 2, -2)
            hidden_down(m - 1, -1)
            for n in range(NB):
                pe.wait_ge(go_sb, n // 2 + 1)
                if n < 2:
                    pe.wait_ge(u_sb, m)
                else:
                    pe.wait_ge(so_sb, n - 1)
                o = banks[n % 2][:, :].rearrange("p (t d) -> p t d", t=TT)
                for t in range(TT):
                    c = (n % 2) * T + t * P
                    for k in range(KD):
                        last = pe.transpose(o[:, t, k * P:(k + 1) * P], g_o[:, k, c:c + P], ident[:])
                last.then_inc(gT_ps, 1)

        @block.scalar
        def _(act):
            raw_ready(act, 0)
            act.activation(wqk_h[:].rearrange("p s k c -> p (s k c)"), raw[:, 0, :], ACT.Copy).then_inc(wa_hi, 1)

            def norm_T0(b):
                act.wait_ge(xT0_ps, b + 1)
                act.activation(xT0h[:].rearrange("p k t -> p (k t)"), banks[0][:, :], ACT.Copy).then_inc(xT0h_sb, 1)

            def group_q(b, g):
                act.wait_ge(qk0_ps, 4 * b + g + 1)
                after(act, qz0_sb, 4 * b + g - 1)
                act.activation(qT0[:, g % 2, :], banks[g % 2][:, 0:T], ACT.Copy, scale=float(E0) ** -0.5)\
                   .then_inc(qT0_sb, 1)

            def exps(b, g):
                act.wait_ge(max0, 8 * b + 2 * g + 2)
                for t in range(TT):
                    for h in range(GH):
                        c = slice(h * P, (h + 1) * P)
                        if t == 0:
                            o, i = pex[:, 0, h, :], trio[:, 0, c]
                        else:
                            o, i = pex[:, 1:3, h, :], trio[:, 1:3, c]
                        last = act.activation(o, i, ACT.Exp, bias=nmax[:, g, t, h:h + 1])
                last.then_inc(exp0, 1)

            def probs_T(b, g):
                after(act, y0_ps, 4 * b + g)
                for i in range(3):
                    n = 3 * g + i
                    act.wait_ge(pT0_ps, 12 * b + n + 1)
                    act.activation(pT0[:, i, :, :].rearrange("p h q -> p (h q)"), more[:, n % 2, :], ACT.Copy)\
                       .then_inc(pT0_sb, 1)

            def gate_tanh(b, j):
                n = {0: 5, 1: 6, 2: 8, 3: 9, 4: 11, 5: 13, 6: 16, 7: 19}[j]
                act.wait_ge(up_ps, 8 * b + j + 1)
                after(act, hid_sb, 8 * b + j - 1)
                act.activation(th0[:, j % 2, :], banks[n % 2][:, 0:T], ACT.Tanh, scale=0.5).then_inc(th0_sb, 1)

            def hidden_hi(b, j):
                act.wait_ge(hid_sb, 8 * b + j + 1)
                after(act, down_ps, 8 * b + j - 3)
                act.activation(hid_h[:, j % 4, :], hid[:, j % 2, :], ACT.Copy).then_inc(hidh_sb, 1)

            def gate_out(b):
                act.wait_ge(down_ps, 8 * b + 8)
                after(act, x1_sb, b)
                act.activation(gate0[:].rearrange("p t d -> p (t d)"), more[:, 2, :], ACT.Tanh, scale=0.5)\
                   .then_inc(thf_sb, 1)

            def norm_T1(b):
                act.wait_ge(xT1_ps, b + 1)
                after(act, xT1_stored, 32 * b)
                after(act, lgT_ps, b)
                act.activation(xT1h_c[:].rearrange("p k t -> p (k t)"), banks[1][:, :], ACT.Copy).then_inc(xT1h_sb, 1)

            def logits_T(b):
                act.wait_ge(lgT_ps, b + 1)
                act.activation(lgT[:], banks[0][:, 0:T], ACT.Copy).then_inc(lgT_sb, 1)

            def logits_tanh(b):
                act.wait_ge(lg_ps, b + 1)
                o = banks[1][:, 0:TT * P].rearrange("p (t e) -> p t e", t=TT)
                act.activation(r_th[:], o[:, :, 0:NE], ACT.Tanh, scale=0.5).then_inc(rth_sb, 1)

            def route_T(b):
                act.wait_ge(probT_ps, b + 1)
                act.activation(probT[:, bass.ds(b * T, T)], banks[0][:, 0:T], ACT.Copy).then_inc(probT_sb, 1)

            def batch(b, first, final):
                t = b - 1
                if not first:
                    gate_out(t)
                for g in range(NG):
                    group_q(b, g)
                act.wait_ge(v0_ps, b + 1)
                after(act, y0_ps, 4 * b)
                act.activation(v0[:, :, :, 0:E0], banks[0][:, :].rearrange("p (t h e) -> p t h e", t=TT, h=H0),
                               ACT.Copy).then_inc(v0_sb, 1)
                exps(b, 0)
                gate_tanh(b, 0)
                gate_tanh(b, 1)
                hidden_hi(b, 0)
                if not first:
                    norm_T1(t)
                hidden_hi(b, 1)
                gate_tanh(b, 2)
                probs_T(b, 0)
                exps(b, 1)
                gate_tanh(b, 3)
                hidden_hi(b, 2)
                hidden_hi(b, 3)
                if first:
                    act.wait_ge(fw_step, 6)
                    act.activation(w2_h[:].rearrange("p j d -> p (j d)"), raw[:, 1, :], ACT.Copy).then_inc(fw_hi, 1)
                    for i in range(4):
                        act.wait_ge(fw_done, i + 1)
                        act.activation(w2_h[:, 2 * i:2 * i + 2, :].rearrange("p j d -> p (j d)"), banks[i % 2][:, :],
                                       ACT.Copy, scale=0.5 * float(FF) ** -0.5).then_inc(w2_hi, 1)
                gate_tanh(b, 4)
                if not first:
                    logits_T(t)
                hidden_hi(b, 4)
                probs_T(b, 1)
                exps(b, 2)
                gate_tanh(b, 5)
                hidden_hi(b, 5)
                if not first:
                    logits_tanh(t)
                probs_T(b, 2)
                exps(b, 3)
                gate_tanh(b, 6)
                hidden_hi(b, 6)
                if not first:
                    route_T(t)
                gate_tanh(b, 7)
                if not final:
                    norm_T0(b + 1)
                hidden_hi(b, 7)
                probs_T(b, 3)
                act.wait_ge(yT0_ps, b + 1)
                act.activation(yT0h[:].rearrange("p k t -> p (k t)"), banks[0][:, :], ACT.Copy).then_inc(yT0h_sb, 1)
                act.wait_ge(o0_ps, b + 1)
                after(act, x1_sb, b)
                act.activation(s0[:].rearrange("p t d -> p (t d)"), banks[1][:, :], ACT.Copy).then_inc(s0_sb, 1)

            act.wait_ge(consts_loaded, 16 * N_CONST)
            norm_T0(0)
            raw_ready(act, 1)
            act.activation(wvo_h[:], raw[:, 1, 0:1280], ACT.Copy).then_inc(wa_hi, 1)
            for n, w in ((2, w1_h), (3, w3_h)):
                raw_ready(act, n)
                act.activation(w[:].rearrange("p k c -> p (k c)"), raw[:, n % 2, :], ACT.Copy).then_inc(wa_hi, 1)
            batch(0, True, False)
            with act.Fori(1, NB - 1) as b:
                batch(b, False, False)
            batch(NB - 1, False, True)
            t = NB - 1
            gate_out(t)
            norm_T1(t)
            logits_T(t)
            logits_tanh(t)
            route_T(t)

            def unit_hi(v, par, q):
                raw_half = (A_LOADS + par) % 2
                if q == 0:
                    act.wait_ge(raw_loaded[raw_half], (v - par) * 8 + 16 * ((A_LOADS + par) // 2 + 1))
                    after(act, o1_ps, NB * (v - 1))
                c = slice(512 * q, 512 * q + 512)
                act.activation(bw_h[:, par, c], raw[:, raw_half, c], ACT.Copy).then_inc(bw_hi, 1)

            def scores_exp(n, i):
                r = i % 2
                act.wait_ge(s1_ps, n + 1)
                act.wait_ge(rstd_sb, n + 1)
                for h in range(2):
                    act.activation(pT1[:, r, h, 0:T], trio[:, 0, h * T:(h + 1) * T], ACT.Tanh,
                                   scale=rstd[:, r, 2 + h:3 + h])
                    last = act.activation(pT1[:, r, h, T:T + P], trio[:, 1, h * P:(h + 1) * P], ACT.Tanh,
                                          scale=rstd[:, r, 6 + h:7 + h])
                last.then_inc(tanh1, 1)

            def step(n, i, first, last_unit, next_unit):
                def live(lag):
                    return not first or i >= lag
                for tt in range(TT):
                    act.wait_ge(qk1_ps, 2 * n + tt + 1)
                    if tt == 0:
                        after(act, qT1_ps, n - 1)
                    act.activation(xs[:, i % 2, tt, :, :, :].rearrange("p s h e -> p (s h e)"), banks[tt][:, :], ACT.Copy).then_inc(xs_sb, 1)
                    after(act, ssq_sb, 2 * n + tt - 1)
                    act.activation(sq[:, tt, :], banks[tt][:, :], ACT.Square).then_inc(sq_sb, 1)
                act.wait_ge(v1_ps, n + 1)
                if first and i == 0:
                    act.wait_ge(v1_ones, 1)
                act.activation(v1[:, i % 4, :, :, 0:E1], banks[0][:, :].rearrange("p (t h e) -> p t h e", t=TT, h=2),
                               ACT.Copy).then_inc(v1_sb, 1)
                if live(1):
                    key_query(n - 1, i - 1)
                    scores_exp(n - 1, i - 1)
                if live(2):
                    out_hi(n - 2, i - 2)
                if live(1):
                    numerators(n - 1, i - 1)
                if not last_unit and 3 <= i % NB < 7:
                    unit_hi(next_unit, (i // NB + 1) % 2, i % NB - 3)

            def key_query(n, i):
                act.wait_ge(qT1_ps, n + 1)
                act.activation(qT1[:, i % 2, :, :].rearrange("p h t -> p (h t)"), trio[:, 2, :], ACT.Copy)\
                   .then_inc(qT1_sb, 1)

            def numerators(n, i):
                act.wait_ge(tanh1, n + 1)
                p = pT1[:, i % 2, :, :].rearrange("p h t -> p (h t)")
                act.activation(p, p, ACT.Exp, scale=CAP).then_inc(exp1, 1)

            def out_hi(n, i):
                act.wait_ge(yT1_ps, n + 1)
                after(act, o1_ps, n - 1)
                act.activation(yT1h[:, i % 2, :, :].rearrange("p h t -> p (h t)"), trio[:, 2, :], ACT.Copy)\
                   .then_inc(yT1h_sb, 1)

            def unit_pair(w, first, final):
                for i in range(2 * NB):
                    step(2 * NB * w + i, i, first, final and i >= NB, 2 * w + i // NB + 1)

            act.wait_ge(probT_sb, NB)
            for q in range(4):
                unit_hi(0, 0, q)
            unit_pair(0, True, False)
            with act.Fori(1, NU // 2 - 1) as w:
                unit_pair(w, False, False)
            unit_pair(NU // 2 - 1, False, True)
            n = NU * NB
            key_query(n - 1, -1)
            scores_exp(n - 1, -1)
            out_hi(n - 2, -2)
            numerators(n - 1, -1)
            out_hi(n - 1, -1)

            def pair_hi(p, par, q):
                raw_half = (A_LOADS + NU + par) % 2
                if q == 0:
                    act.wait_ge(raw_loaded[raw_half], (p - par) * 8 + 16 * ((A_LOADS + NU + par) // 2 + 1))
                    after(act, down1_ps, 8 * (p - 1))
                c = slice(512 * q, 512 * q + 512)
                act.activation(cw_h[:, par, c], raw[:, raw_half, c], ACT.Copy).then_inc(cw_hi, 1)

            def pair_rows(p, par):
                act.activation(rows_cur[:, par, :, :].rearrange("p c h -> p (c h)"),
                               expert_rows[:, bass.ds(2 * P * p, 2 * P)], ACT.Copy).then_inc(rows_made, 1)

            def expert_step(m, i, shared):
                r = i % 2
                act.wait_ge(gate_ps, m + 1)
                after(act, z1_sb, m - 1)
                act.activation(h3[:, r, :], trio[:, r, :], ACT.Copy).then_inc(h3_sb, 1)
                if shared:
                    act.wait_ge(up1_ps, m + 1)
                    act.activation(th1[:, r, :], banks[r][:, :], ACT.Tanh, scale=0.5).then_inc(th1_sb, 1)
                else:
                    act.wait_ge(u_sb, m + 1)
                    act.activation(th1[:, r, :], u[:, r, :], ACT.Tanh, scale=0.5).then_inc(th1_sb, 1)
                act.wait_ge(z1_sb, m + 1)
                after(act, down1_ps, m - 1)
                act.activation(z1h[:, r, :], z1[:, r, :], ACT.Copy).then_inc(z1h_sb, 1)

            def four_chunks(w, final):
                for i in range(16):
                    expert_step(16 * w + i, i, final and i >= 8)
                    if 3 <= i % 8 < 6 and not (final and i >= 8):
                        p, par = 2 * w + i // 8 + 1, (i // 8 + 1) % 2
                        pair_hi(p, par, i % 8 - 3)
                        if i % 8 == 3 and not final:
                            pair_rows(p, par)

            act.wait_ge(acc1, NU * NB)
            act.wait_ge(expert_loaded, 16)
            for q in range(3):
                pair_hi(0, 0, q)
            pair_rows(0, 0)
            four_chunks(0, False)
            with act.Fori(1, NC // 4 - 1) as w:
                four_chunks(w, False)
            four_chunks(NC // 4 - 1, True)
            for n in range(NBLK):
                act.wait_ge(acc_sb, 8 * (C_PAIRS - 1) + 2 * n + 2)
                after(act, go_sb, n)
                act.activation(th_o[:], acc[:, :, n * BLK:(n + 1) * BLK], ACT.Tanh, scale=0.25).then_inc(tho_sb, 1)

        @block.vector
        def _(dve):
            def tile(b, t):
                return xs_all[:, bass.ds(2 * b + t, 1), :].rearrange("p a d -> p (a d)")

            def seq(b):
                return xs_all[:, bass.ds(2 * b, TT), :]

            def f32(ap):
                return ap.bitcast(F32)

            def lo(out, full, hi):
                return dve.tensor_tensor(out=out, in0=full, in1=f32(hi), op=ALU.subtract)

            def stats(b, st, mv, ve, st_sem, mv_sem, ve_sem, x1_ready=None):
                dve.wait_ge(x0_loaded if isinstance(b, int) and b == 0 else x_loaded, 16)
                if x1_ready is not None:
                    dve.wait_ge(x1_sb, x1_ready)
                    dve.tensor_copy(waited[:], ident[:, 0:1])
                for t in range(TT):
                    last = dve.bn_stats(out=st[:, t, :], in_=tile(b, t))
                last.then_inc(st_sem, 1)
                dve.wait_ge(st_sem, b + 1)
                dve.tensor_copy(waited[:], st[:, 0, 0:1])
                for t in range(TT):
                    last = dve.bn_aggr(out=mv[:, t, :], in_=st[:, t, :])
                last.then_inc(mv_sem, 1)
                dve.wait_ge(mv_sem, b + 1)
                dve.tensor_scalar(out=ve[:], in0=mv[:, :, 1], scalar1=LN_EPS, scalar2=None, op0=ALU.add)\
                   .then_inc(ve_sem, 1)

            def normalise(b, xn, mv, rs, rs_sem, xn_sem):
                dve.wait_ge(rs_sem, b + 1)
                for t in range(TT):
                    dve.tensor_scalar(out=xn[:, t, :], in0=tile(b, t), scalar1=mv[:, t, 0:1], scalar2=rs[:, t:t + 1],
                                      op0=ALU.subtract, op1=ALU.mult).then_inc(xn_sem, 1)

            stats(0, st0, mv0, ve0, st0_sb, mv0_sb, ve0_sb)
            raw_ready(dve, 0)
            dve.wait_ge(wa_hi, 1)
            lo(wqk_l[:].rearrange("p s k c -> p (s k c)"), raw[:, 0, :], wqk_h[:].rearrange("p s k c -> p (s k c)"))\
                .then_inc(wa_lo_v, 1)
            normalise(0, xn0, mv0, rs0, rs0_sb, xn0_sb)
            dve.wait_ge(consts_loaded, 16 * N_CONST)
            dve.tensor_copy(ident_b[:], ident[:])
            dve.tensor_copy(tri_add[:], tri_add32[:].unsqueeze(1).to_broadcast([P, GH, P]))
            dve.tensor_copy(hadamard_r[:], hadamard[:])
            dve.tensor_scalar(out=gate_bias[:], in0=gate_bias[:], scalar1=0.5, scalar2=None, op0=ALU.add)\
               .then_inc(consts_made, 1)

            def norm_T0(b):
                dve.wait_ge(xT0h_sb, b + 1)
                lo(xT0l[:].rearrange("p k t -> p (k t)"), banks[0][:, :], xT0h[:].rearrange("p k t -> p (k t)"))\
                    .then_inc(xT0l_sb, 1)

            def group_k(b, g):
                dve.wait_ge(qT0_sb, 4 * b + g + 1)
                dve.tensor_tensor(out=kT0[:, g, :], in0=banks[g % 2][:, T:2 * T], in1=alibi_k[:], op=ALU.add)\
                   .then_inc(qk0_sb, 1)

            def maxima(b, g):
                dve.wait_ge(s0_ps, 4 * b + g + 1)
                dve.tensor_reduce(out=nmax[:, g, 0, :], in_=trio[:, 0, :].rearrange("p (h k) -> p h k", h=GH),
                                  axis=AX.X, op=ALU.max, negate=True).then_inc(max0, 1)
                dve.tensor_reduce(out=nmax[:, g, 1, :], in_=trio[:, 1:3, :].rearrange("p c (h k) -> p h c k", h=GH),
                                  axis=AX.XY, op=ALU.max, negate=True).then_inc(max0, 1)

            def hidden(b, j):
                n = {0: 5, 1: 6, 2: 8, 3: 9, 4: 11, 5: 13, 6: 16, 7: 19}[j]
                r = j % 2
                dve.wait_ge(th0_sb, 8 * b + j + 1)
                dve.scalar_tensor_tensor(out=th0[:, r, :], in0=th0[:, r, :], scalar=1.0, in1=banks[n % 2][:, 0:T],
                                         op0=ALU.add, op1=ALU.mult).then_inc(z0_sb, 1)
                dve.wait_ge(z0_sb, 8 * b + j + 1)
                after(dve, hidl_sb, 8 * b + j - 1)
                dve.tensor_tensor(out=hid[:, r, :], in0=banks[n % 2][:, T:2 * T], in1=th0[:, r, :], op=ALU.mult)\
                   .then_inc(hid_sb, 1)

            def heads_out(b, g):
                n = {0: 10, 1: 14, 2: 17, 3: 21}[g]
                dve.wait_ge(y0_ps, 4 * b + g + 1)
                o = banks[n % 2][:, 0:TT * GH * (E0 + 1)].rearrange("p (t h e) -> p t h e", t=TT, h=GH)
                dve.reciprocal(out=rden0[:, g, :, :], in_=o[:, :, :, E0]).then_inc(rden0_sb, 1)
                dve.wait_ge(rden0_sb, 4 * b + g + 1)
                y = y0[:, :, g * GH * E0:(g + 1) * GH * E0].rearrange("p t (h e) -> p t h e", h=GH)
                dve.tensor_tensor(out=y, in0=o[:, :, :, 0:E0],
                                  in1=rden0[:, g, :, :].unsqueeze(3).to_broadcast([P, TT, GH, E0]), op=ALU.mult)\
                   .then_inc(y0_sb, 1)

            def gate_out(b):
                dve.wait_ge(thf_sb, b + 1)
                flat = gate0[:].rearrange("p t d -> p (t d)")
                dve.scalar_tensor_tensor(out=flat, in0=flat, scalar=1.0, in1=more[:, 2, :], op0=ALU.add, op1=ALU.mult)\
                   .then_inc(gf_sb, 1)

            def gate_s(b):
                dve.wait_ge(gf_sb, b + 1)
                dve.wait_ge(s0_sb, b + 1)
                dve.tensor_tensor(out=gate0[:], in0=gate0[:], in1=s0[:], op=ALU.mult).then_inc(sgf_sb, 1)

            def residual(b):
                dve.wait_ge(sgf_sb, b + 1)
                dve.scalar_tensor_tensor(out=seq(b), in0=gate0[:], scalar=0.5, in1=seq(b), op0=ALU.mult, op1=ALU.add)\
                   .then_inc(x1_sb, 1)

            def norm_T1(b):
                dve.wait_ge(xT1h_sb, b + 1)
                lo(xT1l_c[:].rearrange("p k t -> p (k t)"), banks[1][:, :], xT1h_c[:].rearrange("p k t -> p (k t)"))\
                    .then_inc(xT1l_sb, 1)

            def router(b):
                n = [0]

                def link(ins):
                    n[0] += 1
                    ins.then_inc(route, 1)
                    dve.wait_ge(route, 10 * b + n[0])

                four = [P, TT, NE, NE]
                dve.wait_ge(rth_sb, b + 1)
                link(dve.scalar_tensor_tensor(out=r_sc[:], in0=r_th[:], scalar=0.5,
                                              in1=gate_bias[:].unsqueeze(1).to_broadcast([P, TT, NE]),
                                              op0=ALU.mult, op1=ALU.add))
                other, own = r_sc[:].unsqueeze(2).to_broadcast(four), r_sc[:].unsqueeze(3).to_broadcast(four)
                link(dve.tensor_tensor(out=r_ge[:], in0=other, in1=own, op=ALU.is_ge))
                link(dve.tensor_tensor(out=r_ge[:], in0=r_ge[:], in1=before[:].unsqueeze(1).to_broadcast(four),
                                       op=ALU.mult))
                link(dve.tensor_tensor(out=r_gt[:], in0=other, in1=own, op=ALU.is_gt))
                link(dve.tensor_tensor(out=r_gt[:], in0=r_gt[:], in1=r_ge[:], op=ALU.max))
                link(dve.tensor_reduce(out=r_rank[:], in_=r_gt[:], axis=AX.X, op=ALU.add))
                link(dve.scalar_tensor_tensor(out=r_w[:], in0=r_rank[:], scalar=float(TOPK), in1=r_sc[:],
                                              op0=ALU.is_lt, op1=ALU.mult))
                link(dve.tensor_reduce(out=r_sum[:], in_=r_w[:], axis=AX.X, op=ALU.add))
                link(dve.reciprocal(out=r_sum[:], in_=r_sum[:]))
                link(dve.tensor_tensor(out=r_p[:], in0=r_w[:], in1=r_sum[:].unsqueeze(2).to_broadcast([P, TT, NE]),
                                       op=ALU.mult))
                after(dve, probT_ps, b)
                dve.tensor_copy(r_split[:, :, 0:NE], r_p[:]).then_inc(split_hi, 1)
                dve.wait_ge(split_hi, b + 1)
                lo(r_split[:, :, NE:2 * NE], r_p[:], r_split[:, :, 0:NE]).then_inc(split_sb, 1)

            def hadamard_chunks():
                raw_ready(dve, 4)
                dve.wait_ge(wa_hi, 4)
                dve.wait_ge(wa_lo_p, 2)
                src, n = 0, 0
                for s in (1, 2, 4):
                    i = raw[:, src, :].rearrange("p (g two c) -> p g two c", two=2, c=s * D)
                    o = raw[:, 1 - src, :].rearrange("p (g two c) -> p g two c", two=2, c=s * D)
                    for k, op in enumerate((ALU.add, ALU.subtract)):
                        dve.tensor_tensor(out=o[:, :, k, :], in0=i[:, :, 0, :], in1=i[:, :, 1, :], op=op)\
                           .then_inc(fw_step, 1)
                    n += 2
                    dve.wait_ge(fw_step, n)
                    src = 1 - src
                dve.wait_ge(fw_hi, 1)
                lo(w2_l[:].rearrange("p j d -> p (j d)"), raw[:, 1, :], w2_h[:].rearrange("p j d -> p (j d)"))\
                    .then_inc(fw_lo, 1)
                for i in range(4):
                    dve.wait_ge(w2_hi, i + 1)
                    c = slice(2 * i, 2 * i + 2)
                    dve.scalar_tensor_tensor(out=w2_l[:, c, :].rearrange("p j d -> p (j d)"), in0=banks[i % 2][:, :],
                                             scalar=0.5 * float(FF) ** -0.5,
                                             in1=f32(w2_h[:, c, :]).rearrange("p j d -> p (j d)"),
                                             op0=ALU.mult, op1=ALU.subtract).then_inc(w2_lo, 1)

            def batch(b, first, final):
                t = b - 1
                group_k(b, 0)
                if not first:
                    gate_out(t)
                group_k(b, 1)
                if not first:
                    gate_s(t)
                group_k(b, 2)
                if not first:
                    residual(t)
                group_k(b, 3)
                if not first:
                    stats(t, st1, mv1, ve1, st1_sb, mv1_sb, ve1_sb, b)
                maxima(b, 0)
                if not first:
                    normalise(t, xn1, mv1, rs1, rs1_sb, xn1_sb)
                hidden(b, 0)
                hidden(b, 1)
                if not first:
                    norm_T1(t)
                hidden(b, 2)
                maxima(b, 1)
                hidden(b, 3)
                heads_out(b, 0)
                if first:
                    hadamard_chunks()
                hidden(b, 4)
                maxima(b, 2)
                if not final:
                    stats(b + 1, st0, mv0, ve0, st0_sb, mv0_sb, ve0_sb)
                hidden(b, 5)
                heads_out(b, 1)
                if not first:
                    router(t)
                maxima(b, 3)
                hidden(b, 6)
                heads_out(b, 2)
                if not final:
                    normalise(b + 1, xn0, mv0, rs0, rs0_sb, xn0_sb)
                hidden(b, 7)
                if not final:
                    norm_T0(b + 1)
                heads_out(b, 3)
                dve.wait_ge(yT0h_sb, b + 1)
                lo(yT0l[:].rearrange("p k t -> p (k t)"), banks[0][:, :], yT0h[:].rearrange("p k t -> p (k t)"))\
                    .then_inc(yT0l_sb, 1)

            norm_T0(0)
            raw_ready(dve, 1)
            dve.wait_ge(wa_hi, 2)
            lo(wvo_l[:], raw[:, 1, 0:1280], wvo_h[:]).then_inc(wa_lo_v, 1)
            batch(0, True, False)
            with dve.Fori(1, NB - 1) as b:
                batch(b, False, False)
            batch(NB - 1, False, True)
            t = NB - 1
            gate_out(t)
            gate_s(t)
            residual(t)
            stats(t, st1, mv1, ve1, st1_sb, mv1_sb, ve1_sb, NB)
            normalise(t, xn1, mv1, rs1, rs1_sb, xn1_sb)
            norm_T1(t)
            router(t)

            def unit_lo(v, par, q):
                half = (A_LOADS + par) % 2
                dve.wait_ge(bw_hi, 4 * v + q + 1)
                c = slice(512 * q, 512 * q + 512)
                lo(bw_l[:, par, c], raw[:, half, c], bw_h[:, par, c]).then_inc(bw_lo, 1)

            def squares(n, i, tt):
                dve.wait_ge(sq_sb, 2 * n + tt + 1)
                dve.tensor_reduce(out=ssq[:, i % 2, tt, :], in_=sq[:, tt, :].rearrange("p (h e) -> p h e", h=4),
                                  axis=AX.X, op=ALU.add).then_inc(ssq_sb, 1)

            def mean_squares(n, i):
                dve.wait_ge(ssq_sb, 2 * n + 2)
                dve.tensor_scalar(out=msq[:, i % 2, :], in0=ssq[:, i % 2, :, :].rearrange("p t h -> p (t h)"),
                                  scalar1=1.0 / E1, scalar2=RMS_EPS, op0=ALU.mult, op1=ALU.add).then_inc(msq_sb, 1)

            def key_T(n, i, unit):
                dve.wait_ge(kT1_ps, n + 1)
                dve.tensor_tensor(out=kT1[:, i % 2, :, :], in0=more[:, 2, :].rearrange("p (h t) -> p h t", h=2),
                                  in1=qk_scale[:, bass.ds(2 * unit, 2)].unsqueeze(2).to_broadcast([P, 2, T]),
                                  op=ALU.mult).then_inc(kT1_sb, 1)

            def heads_out1(n, i):
                dve.wait_ge(y1_ps, n + 1)
                o = more[:, 0:2, 0:2 * (E1 + 1)].rearrange("p t (h e) -> p t h e", h=2)
                dve.reciprocal(out=rden1[:, i % 2, :, :], in_=o[:, :, :, E1]).then_inc(rden1_sb, 1)
                dve.wait_ge(rden1_sb, n + 1)
                dve.tensor_tensor(out=y1[:, i % 2, :, :, :], in0=o[:, :, :, 0:E1],
                                  in1=rden1[:, i % 2, :, :].unsqueeze(3).to_broadcast([P, TT, 2, E1]), op=ALU.mult)\
                   .then_inc(y1_sb, 1)

            def add_unit(n, i, first):
                b = i % NB
                dve.wait_ge(o1_ps, n + 1)
                s = s_acc[:, 2 * b:2 * b + 2, :].rearrange("p t d -> p (t d)")
                if first and 0 <= i < NB:
                    dve.tensor_copy(s, banks[1][:, :]).then_inc(acc1, 1)
                else:
                    after(dve, acc1, n + 1 - NB)
                    dve.tensor_tensor(out=s, in0=banks[1][:, :], in1=s, op=ALU.add).then_inc(acc1, 1)

            def out_lo(n, i):
                dve.wait_ge(yT1h_sb, n + 1)
                lo(yT1l[:, i % 2, :, :].rearrange("p h t -> p (h t)"), trio[:, 2, :],
                   yT1h[:, i % 2, :, :].rearrange("p h t -> p (h t)")).then_inc(yT1l_sb, 1)

            def unit_pair(w, first, final):
                for i in range(2 * NB):
                    n = 2 * NB * w + i

                    def live(lag):
                        return not first or i >= lag
                    squares(n, i, 0)
                    squares(n, i, 1)
                    mean_squares(n, i)
                    if live(1):
                        key_T(n - 1, i - 1, 2 * w + (i - 1) // NB)
                    if live(2):
                        heads_out1(n - 2, i - 2)
                    if live(3):
                        add_unit(n - 3, i - 3, first)
                    if live(2):
                        out_lo(n - 2, i - 2)
                    if 3 <= i % NB < 7 and not (final and i >= NB):
                        unit_lo(2 * w + i // NB + 1, (i // NB + 1) % 2, i % NB - 3)

            dve.wait_ge(probT_sb, NB)
            for q in range(4):
                unit_lo(0, 0, q)
            dve.wait_ge(rope_made, 6)
            unit_pair(0, True, False)
            with dve.Fori(1, NU // 2 - 1) as w:
                unit_pair(w, False, False)
            unit_pair(NU // 2 - 1, False, True)
            n = NU * NB
            key_T(n - 1, -1, NU - 1)
            heads_out1(n - 2, -2)
            add_unit(n - 3, -3, False)
            out_lo(n - 2, -2)
            add_unit(n - 2, -2, False)
            heads_out1(n - 1, -1)
            out_lo(n - 1, -1)
            add_unit(n - 1, -1, False)

            def pair_lo(p, par, q):
                half = (A_LOADS + NU + par) % 2
                dve.wait_ge(cw_hi, 3 * p + q + 1)
                c = slice(512 * q, 512 * q + 512)
                lo(cw_l[:, par, c], raw[:, half, c], cw_h[:, par, c]).then_inc(cw_lo, 1)

            def add_pair(m, i, first):
                blk = (i % 8) // 2
                dve.wait_ge(down1_ps, m + 1)
                for k in range(KD):
                    a = acc[:, k, blk * BLK:(blk + 1) * BLK]
                    if first and 0 <= i < 8:
                        dve.tensor_copy(a, more[:, 1 + k, :]).then_inc(acc_sb, 1)
                    else:
                        dve.wait_ge(acc_sb, m - 7)
                        dve.tensor_tensor(out=a, in0=more[:, 1 + k, :], in1=a, op=ALU.add).then_inc(acc_sb, 1)

            def four_chunks(w, first, final):
                for i in range(16):
                    m, r = 16 * w + i, i % 2
                    shared = final and i >= 8
                    if shared:
                        dve.wait_ge(th1_sb, m + 1)
                        dve.scalar_tensor_tensor(out=u[:, r, :], in0=th1[:, r, :], scalar=1.0, in1=banks[r][:, :],
                                                 op0=ALU.add, op1=ALU.mult).then_inc(u_sb, 1)
                    else:
                        dve.wait_ge(up1_ps, m + 1)
                        dve.wait_ge(h3_sb, m + 1)
                        dve.tensor_tensor(out=u[:, r, :], in0=banks[r][:, :], in1=h3[:, r, :], op=ALU.mult)\
                           .then_inc(u_sb, 1)
                        dve.wait_ge(prob_ps, m + 1)
                        dve.wait_ge(u_sb, m + 1)
                        prob = trio[:, 2, :] if r == 0 else more[:, 0, :]
                        dve.tensor_tensor(out=w_u[:, r, :], in0=prob, in1=u[:, r, :], op=ALU.mult).then_inc(wu_sb, 1)
                    if i % 2 == 1 and (not first or i >= 3):
                        add_pair(m - 2, i - 2, first)
                    after(dve, z1l_sb, m - 1)
                    if shared:
                        dve.wait_ge(u_sb, m + 1)
                        dve.wait_ge(h3_sb, m + 1)
                        dve.tensor_tensor(out=z1[:, r, :], in0=u[:, r, :], in1=h3[:, r, :], op=ALU.mult)\
                           .then_inc(z1_sb, 1)
                    else:
                        dve.wait_ge(wu_sb, m + 1)
                        dve.wait_ge(th1_sb, m + 1)
                        dve.scalar_tensor_tensor(out=z1[:, r, :], in0=th1[:, r, :], scalar=1.0, in1=w_u[:, r, :],
                                                 op0=ALU.add, op1=ALU.mult).then_inc(z1_sb, 1)
                    if 3 <= i % 8 < 6 and not shared:
                        pair_lo(2 * w + i // 8 + 1, (i // 8 + 1) % 2, i % 8 - 3)

            for q in range(3):
                pair_lo(0, 0, q)
            four_chunks(0, True, False)
            with dve.Fori(1, NC // 4 - 1) as w:
                four_chunks(w, False, False)
            four_chunks(NC // 4 - 1, False, True)
            add_pair(16 * (NC // 4) - 1, -1, False)
            for n in range(NBLK):
                dve.wait_ge(tho_sb, n + 1)
                after(dve, gT_ps, 2 * n)
                dve.scalar_tensor_tensor(out=g_o[:], in0=th_o[:], scalar=1.0, in1=acc[:, :, n * BLK:(n + 1) * BLK],
                                         op0=ALU.add, op1=ALU.mult).then_inc(go_sb, 1)
                for b in (2 * n, 2 * n + 1):
                    dve.wait_ge(gT_ps, b + 1)
                    s = s_acc[:, 2 * b:2 * b + 2, :].rearrange("p t d -> p (t d)")
                    dve.tensor_tensor(out=s, in0=banks[b % 2][:, :], in1=s, op=ALU.mult).then_inc(so_sb, 1)
                    dve.wait_ge(so_sb, b + 1)
                    xb = xs_all[:, 2 * b:2 * b + 2, :].rearrange("p t d -> p (t d)")
                    dve.scalar_tensor_tensor(out=xb, in0=s, scalar=0.25, in1=xb, op0=ALU.mult, op1=ALU.add)\
                       .then_inc(o_sb_made, 1)

        @block.gpsimd
        def _(pool):
            pool.memset(half_pow[:], -0.5).then_inc(pow_made, 1)
            pool.memset(qz0[:].rearrange("p g h t -> p (g h t)"), 0.0).then_inc(qz0_zero, 1)
            pool.memset(v0[:, :, :, E0:E0 + 1], 1.0).then_inc(pow_made, 1)
            pool.memset(r_split[:].bitcast(F32).rearrange("p t e -> p (t e)"), 0.0).then_inc(pow_made, 1)

            def inverse_root(b, ve, rs, ve_sem, rs_sem):
                pool.wait_ge(ve_sem, b + 1)
                pool.tensor_tensor(out=rs[:], in0=ve[:], in1=half_pow[:, 0:TT], op=ALU.pow).then_inc(rs_sem, 1)

            pool.wait_ge(pow_made, 3)
            pool.wait_ge(consts_loaded, 16 * N_CONST)
            pool.wait_ge(qz0_zero, 1)
            inverse_root(0, ve0, rs0, ve0_sb, rs0_sb)

            def one_head_q(b, g):
                pool.wait_ge(qT0_sb, 4 * b + g + 1)
                after(pool, s0_ps, 4 * (b - 1) + g + 1)
                for h in range(GH):
                    r = slice(HP * h, HP * h + HP)
                    last = pool.tensor_tensor(out=qz0[r, g, h, :], in0=qT0[r, g % 2, :],
                                              in1=alibi_q[r, g:g + 1].to_broadcast([HP, T]), op=ALU.add)
                last.then_inc(qz0_sb, 1)

            def hidden_lo(b, j):
                pool.wait_ge(hidh_sb, 8 * b + j + 1)
                pool.tensor_tensor(out=hid_l[:, j % 4, :], in0=hid[:, j % 2, :], in1=hid_h[:, j % 4, :].bitcast(F32),
                                   op=ALU.subtract).then_inc(hidl_sb, 1)

            def batch(b, first, final):
                t = b - 1
                after(pool, hidl_sb, NJ * b)
                for g in range(NG):
                    one_head_q(b, g)
                pool.wait_ge(qz0_sb, NG * b + NG)
                if not first:
                    inverse_root(t, ve1, rs1, ve1_sb, rs1_sb)
                else:
                    for n, wl, wh in ((2, w1_l, w1_h), (3, w3_l, w3_h)):
                        pool.wait_ge(wa_hi, n + 1)
                        pool.tensor_tensor(out=wl[:].rearrange("p k c -> p (k c)"), in0=raw[:, n % 2, :],
                                           in1=wh[:].bitcast(F32).rearrange("p k c -> p (k c)"), op=ALU.subtract)\
                            .then_inc(wa_lo_p, 1)
                for j in range(5):
                    hidden_lo(b, j)
                if not final:
                    inverse_root(b + 1, ve0, rs0, ve0_sb, rs0_sb)
                for j in range(5, NJ):
                    hidden_lo(b, j)

            batch(0, True, False)
            col = [norm_w[:, s:s + 1].to_broadcast([P, H1]) for s in range(2)]
            pool.tensor_tensor(out=cosT_sb[:], in0=cosT_sb[:], in1=cosT_sb[:], op=ALU.mult).then_inc(rope_made, 1)
            pool.tensor_tensor(out=sinT_sb[:], in0=sinT_sb[:], in1=sinT_sb[:], op=ALU.mult).then_inc(rope_made, 1)
            pool.wait_ge(rope_made, 2)
            pool.tensor_tensor(out=cosT_sb[:], in0=cosT_sb[:], in1=sinT_sb[:], op=ALU.add).then_inc(rope_made, 1)
            pool.wait_ge(rope_made, 3)
            pool.tensor_tensor(out=cosT_sb[:], in0=cosT_sb[:], in1=col[0], op=ALU.mult).then_inc(rope_made, 1)
            pool.wait_ge(rope_made, 4)
            pool.tensor_tensor(out=cosT_sb[:], in0=cosT_sb[:], in1=col[1], op=ALU.mult).then_inc(rope_made, 1)
            pool.wait_ge(rope_made, 5)
            pool.tensor_scalar(out=qk_scale[:], in0=cosT_sb[:], scalar1=float(E1) ** -0.5 / CAP, scalar2=0.0,
                               op0=ALU.mult, op1=ALU.add).then_inc(rope_made, 1)
            pool.wait_ge(rope_made, 6)
            with pool.Fori(1, NB - 1) as b:
                batch(b, False, False)
            batch(NB - 1, False, True)
            t = NB - 1
            inverse_root(t, ve1, rs1, ve1_sb, rs1_sb)

            def norm_q(n, i):
                r = i % 2
                pool.wait_ge(msq_sb, n + 1)
                pool.tensor_tensor(out=rstd[:, r, :], in0=msq[:, r, :], in1=half_pow[:], op=ALU.pow).then_inc(rstd_sb, 1)
                pool.wait_ge(rstd_sb, n + 1)
                for tt in range(TT):
                    last = pool.tensor_tensor(out=qn[:, r, tt, :, :], in0=xs[:, r, tt, 0, :, :],
                                              in1=rstd[:, r, 4 * tt:4 * tt + 2].unsqueeze(2).to_broadcast([P, 2, E1]),
                                              op=ALU.mult)
                last.then_inc(qn_sb, 1)

            def mask(n, i):
                pool.wait_ge(exp1, n + 1)
                p = pT1[:, i % 2, :, :].rearrange("p h (c t) -> p h c t", c=3)[:, :, ::2, :]
                pool.tensor_tensor(out=p, in0=p, in1=tri_mul[:].unsqueeze(1).unsqueeze(1).to_broadcast([P, 2, 2, P]),
                                   op=ALU.mult).then_inc(masked1, 1)

            def unit_pair(w, first):
                for i in range(2 * NB):
                    n = 2 * NB * w + i
                    norm_q(n, i)
                    if not first or i >= 1:
                        mask(n - 1, i - 1)

            pool.wait_ge(probT_sb, NB)
            pool.memset(v1[:].rearrange("p r t h e -> p (r t h) e")[:, :, E1:E1 + 1], 1.0).then_inc(v1_ones, 1)
            unit_pair(0, True)
            with pool.Fori(1, NU // 2) as w:
                unit_pair(w, False)
            mask(NU * NB - 1, -1)

            def four_chunks(w):
                for i in range(16):
                    m, r = 16 * w + i, i % 2
                    pool.wait_ge(z1h_sb, m + 1)
                    pool.tensor_tensor(out=z1l[:, r, :], in0=z1[:, r, :], in1=z1h[:, r, :].bitcast(F32),
                                       op=ALU.subtract).then_inc(z1l_sb, 1)

            with pool.Fori(0, NC // 4) as w:
                four_chunks(w)


def _layouts(x, W_qkv, W_o, W1, W2, W3, wq, wk, wv, wo, gate_w, w1s, w2s, w3s, w1r, w2r, w3r):
    import numpy as np
    f = np.float32

    def chunks(w):
        return w.reshape(w.shape[0] // P, P, w.shape[1]).transpose(1, 0, 2)

    qk = []
    for s in range(2):
        w = np.zeros((D, H0, HP), f)
        w[:, :, :E0] = W_qkv[:, s * D:(s + 1) * D].reshape(D, H0, E0)
        qk.append(chunks(w.reshape(D, H0 * HP)).reshape(P, -1))
    gate = np.zeros((D, P), f)
    gate[:, :NE] = gate_w.T
    vo = [chunks(np.ascontiguousarray(w)).reshape(P, -1) for w in (W_qkv[:, 2 * D:], W_o, gate)]
    attn = []
    for n in range(NU):
        r = slice(2 * E1 * n, 2 * E1 * (n + 1))
        both = np.concatenate([wq[r].T, wk[r].T], 1)
        attn.append(np.concatenate([chunks(both).reshape(P, -1), chunks(np.ascontiguousarray(wv[r].T)).reshape(P, -1),
                                    chunks(np.ascontiguousarray(wo[:, r].T)).reshape(P, -1)], 1))
    up = []
    for routed, shared in ((w1r, w1s), (w3r, w3s)):
        w = np.zeros((D, NC * P), f)
        w[:, :NR * P] = routed.transpose(1, 0, 2).reshape(D, NR * P)
        w[:, NR * P:NR * P + HE] = shared
        up.append(w)
    dn = np.zeros((NC * P, D), f)
    dn[:NR * P] = w2r.reshape(NR * P, D)
    dn[NR * P:NR * P + HE] = w2s
    moe = []
    for n in range(NC // 2):
        c = slice(2 * P * n, 2 * P * (n + 1))
        moe.append(np.concatenate([chunks(np.ascontiguousarray(w[:, c])).reshape(P, -1) for w in up] +
                                  [chunks(dn[c]).reshape(P, -1)], 1))
    return dict(pack_qk=np.concatenate(qk, 1), pack_vo=np.concatenate(vo, 1),
                pack_w1=chunks(np.ascontiguousarray(W1.T)).reshape(P, -1),
                pack_w3=chunks(np.ascontiguousarray(W3.T)).reshape(P, -1),
                pack_w2=chunks(np.ascontiguousarray(W2.T)).reshape(P, -1),
                pack_attn=np.stack(attn), pack_moe=np.stack(moe))


def _rotations(rope_cos, rope_sin):
    import numpy as np
    return {n: np.repeat(np.asarray(v)[:H1].T, 2, axis=0) for n, v in (("rope_cosT", rope_cos), ("rope_sinT", rope_sin))}


def _constants():
    import numpy as np
    f = np.float32
    r = np.arange(P)
    hadamard = np.array([[1.0]])
    while hadamard.shape[0] < P:
        hadamard = np.block([[hadamard, hadamard], [hadamard, -hadamard]])
    slopes = f(2.0) ** (f(-8.0) / np.arange(1, H0 + 1, dtype=f))
    alibi_q, alibi_k = np.zeros((P, NG), f), np.zeros((P, T), f)
    for g in range(NG):
        for h in range(GH):
            alibi_q[HP * h + E0, g] = slopes[g * GH + h]
    for h in range(GH):
        alibi_k[HP * h + E0] = np.arange(T)
    expert_rows = np.zeros((P, NR * P), f)
    expert = np.arange(NR * P) // HE
    expert_rows[expert, np.arange(NR * P)] = 1
    expert_rows[NE + expert, np.arange(NR * P)] = 1
    before = np.broadcast_to((np.arange(NE)[None, :] < np.arange(NE)[:, None]), (P, NE, NE))
    return dict(ident_c=np.eye(P, dtype=f), hadamard_c=hadamard.astype(f),
                tri_add_c=np.where(r[None, :] <= r[:, None], 0.0, -1e30).astype(f),
                tri_mul_c=(r[:, None] <= r[None, :]).astype(f), alibi_q_c=alibi_q, alibi_k_c=alibi_k,
                expert_rows_c=expert_rows, before_c=np.ascontiguousarray(before, f))


def kernel(L0_attn_x, L0_attn_W_qkv, L0_attn_W_o, L0_ffn_W1, L0_ffn_W2, L0_ffn_W3, L1_attn_wq, L1_attn_wk,
           L1_attn_wv, L1_attn_wo, L1_attn_q_norm_w, L1_attn_k_norm_w, L1_attn_rope_cos, L1_attn_rope_sin,
           L1_ffn_gate_w, L1_ffn_gate_b, L1_ffn_w1_shared, L1_ffn_w2_shared, L1_ffn_w3_shared, L1_ffn_w1_routed,
           L1_ffn_w2_routed, L1_ffn_w3_routed):
    import numpy as np
    import concourse.bacc as bacc
    from concourse.bass_utils import run_bass_kernel_spmd

    a = [np.asarray(v) for v in (L0_attn_x, L0_attn_W_qkv, L0_attn_W_o, L0_ffn_W1, L0_ffn_W2, L0_ffn_W3, L1_attn_wq,
                                 L1_attn_wk, L1_attn_wv, L1_attn_wo, L1_ffn_gate_w, L1_ffn_w1_shared, L1_ffn_w2_shared,
                                 L1_ffn_w3_shared, L1_ffn_w1_routed, L1_ffn_w2_routed, L1_ffn_w3_routed)]
    arrays = dict(x=a[0], **_layouts(*a), gate_b=np.asarray(L1_ffn_gate_b), q_norm=np.asarray(L1_attn_q_norm_w)[:, None],
                  k_norm=np.asarray(L1_attn_k_norm_w)[:, None], **_rotations(L1_attn_rope_cos, L1_attn_rope_sin),
                  **_constants())
    arrays = {k: np.ascontiguousarray(v) for k, v in arrays.items()}
    nc = bacc.Bacc("TRN2", target_bir_lowering=False, num_devices=1)
    aps = {k: nc.dram_tensor(k + "_dram", v.shape, F32, kind="ExternalInput").ap() for k, v in arrays.items()}
    out = nc.dram_tensor("out_dram", (NB, T, D), F32, kind="ExternalOutput").ap()
    build(nc, **aps, out=out)
    r = run_bass_kernel_spmd(nc, [{k + "_dram": v for k, v in arrays.items()}], core_ids=[0])
    return r.results[0]["out_dram"]
```

```python
import concourse.bass as bass
from concourse import mybir
from contextlib import ExitStack

F32 = mybir.dt.float32
F32R = mybir.dt.float32r
BF16 = mybir.dt.bfloat16
ALU = mybir.AluOpType
ACT = mybir.ActivationFunctionType
AX = mybir.AxisListType

P = 128
NB, T, D = 8, 256, 256
TT, KD = T // P, D // P
NT = NB * TT
H0, E0 = 16, 16
GH = 4
NG = H0 // GH
GR = GH * E0
KR = GR + 2
FF = 1024
NJ = FF // P
H1, E1 = 16, 128
NU = H1 // 2
CAP = 50.0
NE, TOPK, HE = 16, 4, 176
NR = NE * HE // P
NC = NR + 2
NBLK, BLK = 4, 512
LN_EPS, RMS_EPS = 1e-5, 1e-6


def build(nc, x, pack_qk, pack_vo, pack_w1, pack_w3, pack_w2, pack_attn, pack_moe, gate_b, q_norm, k_norm,
          rope_cosT, rope_sinT, ident_c, hadamard_c, tri_add_c, tri_mul_c, alibi_q_c, alibi_k_c, head_mask_c, before_c, out):
    ctx = ExitStack()
    with ctx:
        def sem(name):
            return ctx.enter_context(nc.semaphore(name))

        def sb(name, shape, dt=F32, stack=ctx):
            return stack.enter_context(nc.sbuf_tensor(name, shape, dt))

        banks = [ctx.enter_context(nc.psum_tensor(f"bank{i}", [P, 512], F32)) for i in range(2)]
        trio = ctx.enter_context(nc.psum_tensor("trio", [P, 3, 512], F32))
        more = ctx.enter_context(nc.psum_tensor("more", [P, 3, 512], F32))

        xs_all = sb("x_all", [P, NT, D])
        probT = sb("probT", [P, NB * T], F32R)
        ident = sb("ident", [P, P])
        raw = sb("raw", [P, 2, 2048])
        qk_scale = sb("qk_scale", [P, H1])
        tri_mul = sb("tri_mul", [P, P])
        half_pow = sb("half_pow", [P, 8])

        a_stack = ExitStack()

        def sa(name, shape, dt=F32):
            return sb(name, shape, dt, a_stack)

        wqk_h, wqk_l = sa("wqk_h", [P, KD, NG * P], F32R), sa("wqk_l", [P, KD, NG * P], F32R)
        w1_h, w1_l = sa("w1_h", [P, KD, FF], F32R), sa("w1_l", [P, KD, FF], F32R)
        w3_h, w3_l = sa("w3_h", [P, KD, FF], F32R), sa("w3_l", [P, KD, FF], F32R)
        w2_h, w2_l = sa("w2_h", [P, NJ, D], F32R), sa("w2_l", [P, NJ, D], F32R)
        w2_a = sa("w2_a", [P, NJ * D])
        hadamard_r = sa("hadamard_r", [P, P], F32R)
        ident_b, tri_add = sa("ident_b", [P, P], BF16), sa("tri_add", [P, GH, P], BF16)
        head_mask = sa("head_mask", [P, GH])
        cosT_sb, sinT_sb, norm_w = sa("cosT_sb", [P, H1]), sa("sinT_sb", [P, H1]), sa("norm_w", [P, 2])
        st0, mv0, ve0, rs0 = sa("st0", [P, TT, 6]), sa("mv0", [P, TT, 2]), sa("ve0", [P, TT]), sa("rs0", [P, TT])
        xn0 = sa("xn0", [P, TT, D])
        xT0h, xT0l = sa("xT0h", [P, KD, T], F32R), sa("xT0l", [P, KD, T], F32R)
        qT0h, qT0l = sa("qT0h", [P, NG, T], F32R), sa("qT0l", [P, NG, T], F32R)
        kT0 = sa("kT0", [P, 2, T])
        kT0h, kT0l = sa("kT0h", [P, NG, T], F32R), sa("kT0l", [P, NG, T], F32R)
        kz0h, kz0l = sa("kz0h", [P, 2, GH, T], F32R), sa("kz0l", [P, 2, GH, T], F32R)
        v0 = sa("v0", [P, TT, H0, E0 + 1])
        nmax = sa("nmax", [P, NG, 2, GH])
        pex = sa("pex", [P, 3, GH, P])
        pT0 = sa("pT0", [P, 3, GH, P])
        rden0 = sa("rden0", [P, NG, TT, GH])
        y0 = sa("y0", [P, TT, D])
        th0, hid = sa("th0", [P, 2, T]), sa("hid", [P, 2, T])
        hid_h, hid_l = sa("hid_h", [P, 4, T], F32R), sa("hid_l", [P, 4, T], F32R)
        wvo_h, wvo_l = sa("wvo_h", [P, 1280], F32R), sa("wvo_l", [P, 1280], F32R)
        yT0h, yT0l = sa("yT0h", [P, KD, T], F32R), sa("yT0l", [P, KD, T], F32R)
        s0 = sa("s0", [P, TT, D])
        st1, mv1, ve1, rs1 = sa("st1", [P, TT, 6]), sa("mv1", [P, TT, 2]), sa("ve1", [P, TT]), sa("rs1", [P, TT])
        waited = sa("waited", [P, 1])
        xn1 = sa("xn1", [P, TT, D])
        gate0 = sa("gate0", [P, TT, D])
        xT1h_c, xT1l_c = sa("xT1h_c", [P, KD, T], F32R), sa("xT1l_c", [P, KD, T], F32R)
        gate_bias, before = sa("gate_bias", [P, NE]), sa("before", [P, NE, NE])
        lgT = sa("lgT", [P, T])
        r_th, r_sc = sa("r_th", [P, TT, NE]), sa("r_sc", [P, TT, NE])
        r_gt, r_ge = sa("r_gt", [P, TT, NE, NE]), sa("r_ge", [P, TT, NE, NE])
        r_rank, r_w = sa("r_rank", [P, TT, NE]), sa("r_w", [P, TT, NE])
        r_sum, r_p = sa("r_sum", [P, TT]), sa("r_p", [P, TT, NE])
        r_split = sa("r_split", [P, TT, P], F32R)
        a_stack.close()

        b_stack = ExitStack()

        def sbb(name, shape, dt=F32):
            return sb(name, shape, dt, b_stack)

        xT1h = sb("xT1h", [P, KD, NB * T], F32R)
        xT1l = sb("xT1l", [P, KD, NB * T], F32R)
        s_acc = sb("s_acc", [P, NT, D])
        rows_cur = sb("rows_cur", [P, 2, 2, P], F32R)
        cw_h, cw_l = sb("cw_h", [P, 2, 1536], F32R), sb("cw_l", [P, 2, 1536], F32R)
        bw_h, bw_l = sbb("bw_h", [P, 2, 2048], F32R), sbb("bw_l", [P, 2, 2048], F32R)
        xs = sbb("xs", [P, 2, TT, 2, 2, E1])
        sq = sbb("sq", [P, TT, 512])
        qn = sbb("qn", [P, 2, TT, 2, E1])
        ssq, msq, rstd = sbb("ssq", [P, 2, TT, 4]), sbb("msq", [P, 2, 8]), sbb("rstd", [P, 2, 8])
        v1 = sbb("v1", [P, 4, TT, 2, E1 + 1])
        qT1, kT1 = sbb("qT1", [P, 2, 2, T]), sbb("kT1", [P, 2, 2, T])
        pT1 = sbb("pT1", [P, 2, 2, 3 * P])
        rden1 = sbb("rden1", [P, 2, TT, 2])
        y1 = sbb("y1", [P, 2, TT, 2, E1])
        yT1h, yT1l = sbb("yT1h", [P, 2, 2, T], F32R), sbb("yT1l", [P, 2, 2, T], F32R)
        b_stack.close()

        acc = sb("acc", [P, KD, NB * T])
        h3, u, th1 = sb("h3", [P, 2, BLK]), sb("u", [P, 2, BLK]), sb("th1", [P, 2, BLK])
        w_u, z1 = sb("w_u", [P, 2, BLK]), sb("z1", [P, 2, BLK])
        z1h, z1l = sb("z1h", [P, 2, BLK], F32R), sb("z1l", [P, 2, BLK], F32R)
        th_o, g_o = sb("th_o", [P, KD, BLK]), sb("g_o", [P, KD, BLK])
        xT1_dram = nc.dram_tensor("xT1_scratch", [2, NB, P, KD * T], F32).ap()

        x0_loaded, x_loaded, consts_loaded = sem("x0_loaded"), sem("x_loaded"), sem("consts_loaded")
        ident_loaded, w2_loaded = sem("ident_loaded"), sem("w2_loaded")
        raw_loaded = [sem("raw_loaded0"), sem("raw_loaded1")]
        out_stored = sem("out_stored")
        consts_made, rope_made, pow_made = sem("consts_made"), sem("rope_made"), sem("pow_made")
        wa_hi, wa_lo = sem("wa_hi"), sem("wa_lo")
        fw_step, fw_hi, fw_lo, fw_done, w2_hi, w2_lo = (sem(n) for n in (
            "fw_step", "fw_hi", "fw_lo", "fw_done", "w2_hi", "w2_lo"))
        xT0_ps, qk0_ps, v0_ps, s0_ps, pT0_ps, y0_ps, yT0_ps, o0_ps, up_ps, down_ps = (sem(n) for n in (
            "xT0_ps", "qk0_ps", "v0_ps", "s0_ps", "pT0_ps", "y0_ps", "yT0_ps", "o0_ps", "up_ps", "down_ps"))
        xT1_ps, lgT_ps, lg_ps, probT_ps = (sem(n) for n in ("xT1_ps", "lgT_ps", "lg_ps", "probT_ps"))
        xT0h_sb, v0_sb, exp0, pT0_sb, yT0h_sb, s0_sb, th0_sb, hidh_sb = (sem(n) for n in (
            "xT0h_sb", "v0_sb", "exp0", "pT0_sb", "yT0h_sb", "s0_sb", "th0_sb", "hidh_sb"))
        thf_sb, xT1h_sb, lgT_sb, rth_sb, probT_sb = (sem(n) for n in (
            "thf_sb", "xT1h_sb", "lgT_sb", "rth_sb", "probT_sb"))
        kT0_sb, kT0h_sb, kT0l_sb, qT0h_sb, qT0l_sb, kz0h_sb, kz0l_sb, alibi_hi, alibi_lo, xT1_stored = (sem(n) for n in (
            "kT0_sb", "kT0h_sb", "kT0l_sb", "qT0h_sb", "qT0l_sb", "kz0h_sb", "kz0l_sb", "alibi_hi", "alibi_lo", "xT1_stored"))
        xT1_loaded = [sem(f"xT1_loaded{b}") for b in range(NB)]
        st0_sb, mv0_sb, ve0_sb, rs0_sb, xn0_sb = (sem(n) for n in ("st0_sb", "mv0_sb", "ve0_sb", "rs0_sb", "xn0_sb"))
        st1_sb, mv1_sb, ve1_sb, rs1_sb, xn1_sb = (sem(n) for n in ("st1_sb", "mv1_sb", "ve1_sb", "rs1_sb", "xn1_sb"))
        xT0l_sb, xT1l_sb, max0, z0_sb, hid_sb, hidl_sb = (sem(n) for n in (
            "xT0l_sb", "xT1l_sb", "max0", "z0_sb", "hid_sb", "hidl_sb"))
        rden0_sb, y0_sb, yT0l_sb, gf_sb, sgf_sb, x1_sb, route, split_sb = (sem(n) for n in (
            "rden0_sb", "y0_sb", "yT0l_sb", "gf_sb", "sgf_sb", "x1_sb", "route", "split_sb"))
        split_hi = sem("split_hi")
        qk1_ps, v1_ps, qT1_ps, kT1_ps, s1_ps, y1_ps, yT1_ps, o1_ps = (sem(n) for n in (
            "qk1_ps", "v1_ps", "qT1_ps", "kT1_ps", "s1_ps", "y1_ps", "yT1_ps", "o1_ps"))
        xs_sb, sq_sb, v1_sb, qT1_sb, tanh1, exp1, yT1h_sb, bw_hi = (sem(n) for n in (
            "xs_sb", "sq_sb", "v1_sb", "qT1_sb", "tanh1", "exp1", "yT1h_sb", "bw_hi"))
        ssq_sb, msq_sb, rstd_sb, qn_sb, masked1 = (sem(n) for n in ("ssq_sb", "msq_sb", "rstd_sb", "qn_sb", "masked1"))
        kT1_sb, rden1_sb, y1_sb, yT1l_sb, acc1, bw_lo, v1_ones = (sem(n) for n in (
            "kT1_sb", "rden1_sb", "y1_sb", "yT1l_sb", "acc1", "bw_lo", "v1_ones"))
        up1_ps, gate_ps, prob_ps, down1_ps, gT_ps = (sem(n) for n in ("up1_ps", "gate_ps", "prob_ps", "down1_ps", "gT_ps"))
        h3_sb, u_sb, th1_sb, wu_sb, z1_sb, z1h_sb, z1l_sb, acc_sb = (sem(n) for n in (
            "h3_sb", "u_sb", "th1_sb", "wu_sb", "z1_sb", "z1h_sb", "z1l_sb", "acc_sb"))
        cw_hi, cw_lo, rows_made, tho_sb, go_sb, so_sb, o_sb_made = (sem(n) for n in (
            "cw_hi", "cw_lo", "rows_made", "tho_sb", "go_sb", "so_sb", "o_sb_made"))

        N_CONST = 12

        def after(eng, s, value):
            if isinstance(value, int) and value <= 0:
                return
            eng.wait_ge(s, value)

        A_LOADS, C_PAIRS = 4, NC // 2

        def raw_ready(eng, n):
            eng.wait_ge(raw_loaded[n % 2], 16 * (n // 2 + 1))

        UP_BANK = (1, 0, 1, 1, 1, 1, 0, 1)
        MIX_BANK = (0, 0, 1, 1)

        hadamard, tri_add32 = y0[:, 0, 0:P], y0[:, 0, P:2 * P]
        alibi_q = pex[GR:KR, 0:2, :, :].rearrange("p c h t -> p (c h t)")
        alibi_k = xs_all[GR:KR, NT // 2:NT, :].rearrange("p t d -> p (t d)")

        block = ctx.enter_context(nc.Block())

        @block.sync
        def _(sp):
            sp.dma_start(xs_all[:, 0:TT, :], x[0].rearrange("(t p) d -> p t d", p=P)).then_inc(x0_loaded, 16)
            sp.dma_start(ident[:], ident_c).then_inc(ident_loaded, 16)
            sp.dma_start(raw[:, 0, 0:KD * NG * P], pack_qk).then_inc(raw_loaded[0], 16)
            sp.dma_start(raw[:, 1, 0:1280], pack_vo).then_inc(raw_loaded[1], 16)
            for dst, src in ((head_mask, head_mask_c), (tri_add32, tri_add_c),
                             (hadamard, hadamard_c), (tri_mul, tri_mul_c), (before, before_c)):
                sp.dma_start(dst[:], src).then_inc(consts_loaded, 16)
            sp.dma_start(alibi_q, alibi_q_c).then_inc(consts_loaded, 16)
            sp.dma_start(alibi_k, alibi_k_c).then_inc(consts_loaded, 16)
            sp.dma_start(gate_bias[:], gate_b.partition_broadcast(P)).then_inc(consts_loaded, 16)
            sp.dma_start(norm_w[:, 0:1], q_norm).then_inc(consts_loaded, 16)
            sp.dma_start(norm_w[:, 1:2], k_norm).then_inc(consts_loaded, 16)
            sp.dma_start(cosT_sb[:], rope_cosT).then_inc(consts_loaded, 16)
            sp.dma_start(sinT_sb[:], rope_sinT).then_inc(consts_loaded, 16)
            sp.wait_ge(wa_hi, 1)
            sp.wait_ge(wa_lo, 1)
            sp.dma_start(raw[:, 0, :], pack_w1).then_inc(raw_loaded[0], 16)
            sp.wait_ge(wa_hi, 2)
            sp.wait_ge(wa_lo, 2)
            sp.dma_start(raw[:, 1, :], pack_w3).then_inc(raw_loaded[1], 16)
            sp.dma_start(w2_a[:], pack_w2).then_inc(w2_loaded, 16)
            sp.dma_start(xs_all[:, TT:NT // 2, :],
                         x[1:NB // 2].rearrange("b (t p) d -> p (b t) d", p=P)).then_inc(x_loaded, 16)
            sp.wait_ge(fw_step, 4)
            sp.dma_start(xs_all[:, NT // 2:NT, :],
                         x[NB // 2:NB].rearrange("b (t p) d -> p (b t) d", p=P)).then_inc(x_loaded, 16)
            sp.wait_ge(wa_hi, 4)
            sp.wait_ge(wa_lo, 4)
            sp.wait_ge(fw_lo, 1)
            for n in range(2):
                sp.dma_start(raw[:, (A_LOADS + n) % 2, :], pack_attn[n]).then_inc(raw_loaded[(A_LOADS + n) % 2], 16)

            def store_norm(b):
                sp.wait_ge(xT1l_sb, b + 1)
                for s, part in enumerate((xT1h_c, xT1l_c)):
                    sp.dma_start(xT1_dram[s, bass.ds(b, 1)].rearrange("a p n -> p (a n)"),
                                 part[:].bitcast(F32).rearrange("p k t -> p (k t)")).then_inc(xT1_stored, 16)

            def load_norm(b):
                sp.wait_ge(xT1_stored, 32 * (b + 1) if b == NB - 1 else 32 * (NB - 1))
                for s, part in enumerate((xT1h, xT1l)):
                    sp.dma_start(part[:, :, b * T:(b + 1) * T].bitcast(F32),
                                 xT1_dram[s, b].rearrange("p (k t) -> p k t", k=KD)).then_inc(xT1_loaded[b], 16)

            with sp.Fori(0, NB - 1) as b:
                store_norm(b)
            sp.wait_ge(yT0_ps, NB)
            for b in range(NB - 1):
                load_norm(b)
            store_norm(NB - 1)
            load_norm(NB - 1)
            with sp.Fori(0, NU // 2 - 1) as w:
                for n in range(2):
                    sp.wait_ge(bw_hi, 4 * (2 * w + n + 1))
                    sp.wait_ge(bw_lo, 4 * (2 * w + n + 1))
                    half = (A_LOADS + n) % 2
                    sp.dma_start(raw[:, half, :], pack_attn[bass.ds(2 * w + n + 2, 1)].rearrange("a p n -> p (a n)"))\
                      .then_inc(raw_loaded[half], 16)
            for n in range(2):
                sp.wait_ge(bw_hi, 4 * (NU - 1 + n))
                sp.wait_ge(bw_lo, 4 * (NU - 1 + n))
                half = (A_LOADS + NU + n) % 2
                sp.dma_start(raw[:, half, 0:1792], pack_moe[n]).then_inc(raw_loaded[half], 16)
            with sp.Fori(0, C_PAIRS // 2 - 1) as w:
                for n in range(2):
                    sp.wait_ge(cw_hi, 3 * (2 * w + n + 1))
                    sp.wait_ge(cw_lo, 3 * (2 * w + n + 1))
                    sp.wait_ge(rows_made, 2 * w + n + 1)
                    half = (A_LOADS + NU + n) % 2
                    sp.dma_start(raw[:, half, 0:1792],
                                 pack_moe[bass.ds(2 * w + n + 2, 1)].rearrange("a p n -> p (a n)"))\
                      .then_inc(raw_loaded[half], 16)
            for n in range(NT // 2):
                sp.wait_ge(o_sb_made, n + 1)
                sp.dma_start(out[n].rearrange("(t p) d -> p t d", p=P), xs_all[:, 2 * n:2 * n + 2, :])\
                  .then_inc(out_stored, 16)
            sp.wait_ge(out_stored, 16 * (NT // 2))

        @block.tensor
        def _(pe):
            def three(o, wh, wl, mh, ml, first, last):
                pe.matmul(o, wh, mh, start=first, stop=False)
                pe.matmul(o, wl, mh, start=False, stop=False)
                return pe.matmul(o, wh, ml, start=False, stop=last)

            def norm_T0(b):
                pe.wait_ge(xn0_sb, 2 * b + 2)
                o = banks[0][:, :].rearrange("p (k t) -> p k t", k=KD)
                for t in range(TT):
                    for k in range(KD):
                        last = pe.transpose(o[:, k, t * P:(t + 1) * P], xn0[:, t, k * P:(k + 1) * P], ident[:])
                last.then_inc(xT0_ps, 1)

            def up(b, j):
                n = UP_BANK[j]
                o = banks[n][:, :].rearrange("p (g t) -> p g t", g=2)
                for g, (wh, wl) in enumerate(((w1_h, w1_l), (w3_h, w3_l))):
                    for k in range(KD):
                        last = three(o[:, g, :], wh[:, k, j * P:(j + 1) * P], wl[:, k, j * P:(j + 1) * P],
                                     xT0h[:, k, :], xT0l[:, k, :], k == 0, k == KD - 1)
                last.then_inc(up_ps, 1)

            def scores(b, g):
                if g == 0:
                    pe.wait_ge(kz0h_sb, b + 1)
                pe.wait_ge(kz0l_sb, 4 * b + g + 1)
                pe.wait_ge(qT0l_sb, 2 * b + g // 2 + 1)
                after(pe, exp0, 4 * b + g)
                for i, (qt, kt) in enumerate(((0, 0), (1, 0), (1, 1))):
                    o, c = trio[:, i, :], slice(qt * P, (qt + 1) * P)
                    q = [v[0:KR, g, c] for v in (qT0h, qT0l)]
                    k = [v[0:KR, g % 2, :, kt * P:(kt + 1) * P] for v in (kz0h, kz0l)]
                    if qt == kt:
                        pe.matmul(o, ident_b[:], tri_add[:].rearrange("p h k -> p (h k)"), start=True, stop=False)
                    o = o.rearrange("p (h k) -> p h k", h=GH)
                    pe.matmul(o, q[0], k[0], start=qt != kt, stop=False)
                    pe.matmul(o, q[0], k[1], start=False, stop=False)
                    last = pe.matmul(o, q[1], k[0], start=False, stop=True)
                last.then_inc(s0_ps, 1)

            def probs_T(b, g, blocks):
                pe.wait_ge(exp0, 4 * b + g + 1)
                for i in blocks:
                    n = 3 * g + i
                    after(pe, pT0_sb, 12 * b + n - 1)
                    o = more[:, n % 2, :].rearrange("p (h q) -> p h q", h=GH)
                    for h in range(GH):
                        last = pe.transpose(o[:, h, :], pex[:, i, h, :], ident[:])
                    last.then_inc(pT0_ps, 1)

            def mix(b, g):
                n = MIX_BANK[g]
                pe.wait_ge(pT0_sb, 12 * b + 3 * g + 3)
                if g == 0:
                    pe.wait_ge(v0_sb, b + 1)
                o = banks[n][:, 0:TT * GH * (E0 + 1)].rearrange("p (t h e) -> p t h e", t=TT, h=GH)
                for h in range(GH):
                    hh = g * GH + h
                    pe.matmul(o[:, 0, h, :], pT0[:, 0, h, :], v0[:, 0, hh, :], start=True, stop=True)
                    pe.matmul(o[:, 1, h, :], pT0[:, 1, h, :], v0[:, 0, hh, :], start=True, stop=False)
                    last = pe.matmul(o[:, 1, h, :], pT0[:, 2, h, :], v0[:, 1, hh, :], start=False, stop=True)
                last.then_inc(y0_ps, 1)

            def down(b, j):
                pe.wait_ge(hidl_sb, 8 * b + j + 1)
                o = more[:, 2, :].rearrange("p (t d) -> p t d", t=TT)
                for t in range(TT):
                    c = slice(t * P, (t + 1) * P)
                    pe.matmul(o[:, t, :], hid_h[:, j % 4, c], w2_h[:, j, :], start=(j == 0 and t == 0), stop=False,
                              skip_group_check=True)
                    pe.matmul(o[:, t, :], hid_l[:, j % 4, c], w2_h[:, j, :], start=False, stop=False, skip_group_check=True)
                    last = pe.matmul(o[:, t, :], hid_h[:, j % 4, c], w2_l[:, j, :], start=False, stop=j == NJ - 1,
                                     skip_group_check=True)
                last.then_inc(down_ps, 1)

            def norm_T1(b, n=0):
                pe.wait_ge(xn1_sb, 2 * b + 2)
                o = banks[n][:, :].rearrange("p (k t) -> p k t", k=KD)
                for t in range(TT):
                    for k in range(KD):
                        last = pe.transpose(o[:, k, t * P:(t + 1) * P], xn1[:, t, k * P:(k + 1) * P], ident[:])
                last.then_inc(xT1_ps, 1)

            def logits_T(b, n=0):
                pe.wait_ge(xT1l_sb, b + 1)
                gate = [w[:, 1024:1280].rearrange("p (k e) -> p k e", k=KD) for w in (wvo_h, wvo_l)]
                for k in range(KD):
                    last = three(banks[n][:, 0:T], gate[0][:, k, :], gate[1][:, k, :], xT1h_c[:, k, :], xT1l_c[:, k, :],
                                 k == 0, k == KD - 1)
                last.then_inc(lgT_ps, 1)

            def logits(b):
                pe.wait_ge(lgT_sb, b + 1)
                for t in range(TT):
                    last = pe.transpose(banks[1][:, t * P:(t + 1) * P], lgT[:, t * P:(t + 1) * P], ident[:])
                last.then_inc(lg_ps, 1)

            def route_T(b, n=0):
                pe.wait_ge(split_sb, b + 1)
                for t in range(TT):
                    last = pe.transpose(banks[n][:, t * P:(t + 1) * P], r_split[:, t, :].bitcast(F32), ident[:])
                last.then_inc(probT_ps, 1)

            def out_T(b):
                pe.wait_ge(y0_sb, 4 * b + 4)
                o = banks[0][:, :].rearrange("p (k t) -> p k t", k=KD)
                for tt in range(TT):
                    for k in range(KD):
                        last = pe.transpose(o[:, k, tt * P:(tt + 1) * P], y0[:, tt, k * P:(k + 1) * P], ident[:])
                last.then_inc(yT0_ps, 1)

            def project_out(b):
                pe.wait_ge(yT0l_sb, b + 1)
                o = banks[0][:, :].rearrange("p (t d) -> p t d", t=TT)
                wo = [w[:, 512:1024].rearrange("p (k d) -> p k d", k=KD) for w in (wvo_h, wvo_l)]
                for tt in range(TT):
                    for k in range(KD):
                        c = slice(tt * P, (tt + 1) * P)
                        pe.matmul(o[:, tt, :], yT0h[:, k, c], wo[0][:, k, :], start=k == 0, stop=False)
                        pe.matmul(o[:, tt, :], yT0l[:, k, c], wo[0][:, k, :], start=False, stop=False)
                        last = pe.matmul(o[:, tt, :], yT0h[:, k, c], wo[1][:, k, :], start=False, stop=k == KD - 1)
                last.then_inc(o0_ps, 1)

            def queries_keys(b, pair):
                o = banks[1][:, :].rearrange("p (g t) -> p g t", g=2)
                for n in range(2):
                    c = slice((2 * pair + n) * P, (2 * pair + n + 1) * P)
                    for k in range(KD):
                        last = three(o[:, n, :], wqk_h[:, k, c], wqk_l[:, k, c], xT0h[:, k, :], xT0l[:, k, :],
                                     k == 0, k == KD - 1)
                last.then_inc(qk0_ps, 1)

            def values(b):
                o = banks[0][:, :].rearrange("p (t d) -> p t d", t=TT)
                wv = [w[:, 0:512].rearrange("p (k d) -> p k d", k=KD) for w in (wvo_h, wvo_l)]
                for tt in range(TT):
                    for k in range(KD):
                        c = slice(tt * P, (tt + 1) * P)
                        pe.matmul(o[:, tt, :], xT0h[:, k, c], wv[0][:, k, :], start=k == 0, stop=False)
                        pe.matmul(o[:, tt, :], xT0l[:, k, c], wv[0][:, k, :], start=False, stop=False)
                        last = pe.matmul(o[:, tt, :], xT0h[:, k, c], wv[1][:, k, :], start=False, stop=k == KD - 1)
                last.then_inc(v0_ps, 1)

            def batch(b, first, final):
                t = b - 1
                pe.wait_ge(xT0l_sb, b + 1)
                if first:
                    pe.wait_ge(wa_lo, 1)
                queries_keys(b, 0)
                if not first:
                    project_out(t)
                pe.wait_ge(qT0l_sb, 2 * b + 1)
                queries_keys(b, 1)
                after(pe, s0_sb, b)
                if first:
                    pe.wait_ge(wa_lo, 2)
                values(b)
                if first:
                    pe.wait_ge(consts_made, 1)
                    pe.wait_ge(alibi_lo, 2)
                scores(b, 0)
                if first:
                    pe.wait_ge(wa_lo, 4)
                pe.wait_ge(qT0l_sb, 2 * b + 2)
                up(b, 0)
                pe.wait_ge(v0_sb, b + 1)
                up(b, 1)
                pe.wait_ge(hid_sb, 8 * b + 1)
                up(b, 2)
                scores(b, 1)
                probs_T(b, 0, (0, 1))
                pe.wait_ge(hid_sb, 8 * b + 3)
                up(b, 3)
                probs_T(b, 0, (2,))
                if not first:
                    norm_T1(t)
                if first:
                    mix(b, 0)
                    pe.wait_ge(hid_sb, 4)
                    up(b, 4)
                    pe.wait_ge(fw_lo, 1)
                    pe.wait_ge(y0_sb, 1)
                    pe.wait_ge(hid_sb, 5)
                    for i in range(4):
                        if i >= 2:
                            pe.wait_ge(w2_lo, i - 1)
                        c = slice(2 * i, 2 * i + 2)
                        o = banks[i % 2][:, :].rearrange("p (j d) -> p j d", j=2)
                        pe.matmul(o, hadamard_r[:], w2_h[:, c, :], start=True, stop=False)
                        pe.matmul(o, hadamard_r[:], w2_l[:, c, :], start=False, stop=True).then_inc(fw_done, 1)
                    pe.wait_ge(w2_lo, 4)
                after(pe, gf_sb, b)
                down(b, 0)
                down(b, 1)
                if not first:
                    pe.wait_ge(xT1l_sb, b)
                    mix(b, 0)
                    pe.wait_ge(hid_sb, 8 * b + 4)
                    up(b, 4)
                pe.wait_ge(y0_sb, 4 * b + 1)
                if not first:
                    logits_T(t)
                scores(b, 2)
                probs_T(b, 1, (0, 1))
                pe.wait_ge(hid_sb, 8 * b + 5)
                up(b, 5)
                probs_T(b, 1, (2,))
                down(b, 2)
                after(pe, lgT_sb, b)
                mix(b, 1)
                down(b, 3)
                pe.wait_ge(hid_sb, 8 * b + 6)
                if not first:
                    logits(t)
                scores(b, 3)
                probs_T(b, 2, (0, 1))
                pe.wait_ge(y0_sb, 4 * b + 2)
                up(b, 6)
                probs_T(b, 2, (2,))
                down(b, 4)
                after(pe, rth_sb, b)
                mix(b, 2)
                down(b, 5)
                pe.wait_ge(hid_sb, 8 * b + 7)
                if not first:
                    route_T(t)
                probs_T(b, 3, (0, 1))
                pe.wait_ge(y0_sb, 4 * b + 3)
                up(b, 7)
                probs_T(b, 3, (2,))
                after(pe, probT_sb, b)
                if not final:
                    norm_T0(b + 1)
                down(b, 6)
                pe.wait_ge(hid_sb, 8 * b + 8)
                mix(b, 3)
                down(b, 7)
                if not final:
                    pe.wait_ge(xT0l_sb, b + 2)
                out_T(b)

            pe.wait_ge(ident_loaded, 16)
            norm_T0(0)
            batch(0, True, False)
            with pe.Fori(1, NB - 1) as b:
                batch(b, False, False)
            batch(NB - 1, False, True)
            t = NB - 1
            project_out(t)

            tr = [trio[:, 2, :], more[:, 2, :]]
            s_b = trio[:, 0:2, :]
            y_b = more[:, 0:2, :]

            def project_qk(n, i, tt):
                b, par = i % NB, (i // NB) % 2
                w = [v[:, par, 0:1024].rearrange("p (k c) -> p k c", k=KD) for v in (bw_h, bw_l)]
                c = slice(b * T + tt * P, b * T + (tt + 1) * P)
                for k in range(KD):
                    pe.matmul(banks[tt][:, :], xT1h[:, k, c], w[0][:, k, :], start=k == 0, stop=False)
                    pe.matmul(banks[tt][:, :], xT1l[:, k, c], w[0][:, k, :], start=False, stop=False)
                    last = pe.matmul(banks[tt][:, :], xT1h[:, k, c], w[1][:, k, :], start=False, stop=k == KD - 1)
                last.then_inc(qk1_ps, 1)

            def project_v(n, i):
                b, par = i % NB, (i // NB) % 2
                w = [v[:, par, 1024:1536].rearrange("p (k c) -> p k c", k=KD) for v in (bw_h, bw_l)]
                o = banks[0][:, :].rearrange("p (t c) -> p t c", t=TT)
                for tt in range(TT):
                    c = slice(b * T + tt * P, b * T + (tt + 1) * P)
                    for k in range(KD):
                        pe.matmul(o[:, tt, :], xT1h[:, k, c], w[0][:, k, :], start=k == 0, stop=False)
                        pe.matmul(o[:, tt, :], xT1l[:, k, c], w[0][:, k, :], start=False, stop=False)
                        last = pe.matmul(o[:, tt, :], xT1h[:, k, c], w[1][:, k, :], start=False, stop=k == KD - 1)
                last.then_inc(v1_ps, 1)

            def transposes_qk(n, i):
                r = i % 2
                pe.wait_ge(xs_sb, 2 * n + 2)
                o = tr[1].rearrange("p (h t) -> p h t", h=2)
                for tt in range(TT):
                    for h in range(2):
                        last = pe.transpose(o[:, h, tt * P:(tt + 1) * P], xs[:, r, tt, 1, h, :], ident[:])
                last.then_inc(kT1_ps, 1)
                pe.wait_ge(qn_sb, n + 1)
                o = tr[0].rearrange("p (h t) -> p h t", h=2)
                for tt in range(TT):
                    for h in range(2):
                        last = pe.transpose(o[:, h, tt * P:(tt + 1) * P], qn[:, r, tt, h, :], ident[:])
                last.then_inc(qT1_ps, 1)

            def scores1(n, i):
                r = i % 2
                pe.wait_ge(qT1_sb, n + 1)
                pe.wait_ge(kT1_sb, n + 1)
                after(pe, tanh1, n)
                for h in range(2):
                    pe.matmul(s_b[:, 0, h * T:(h + 1) * T], kT1[:, r, h, 0:P], qT1[:, r, h, :], start=True, stop=True)
                    last = pe.matmul(s_b[:, 1, h * P:(h + 1) * P], kT1[:, r, h, P:T], qT1[:, r, h, P:T],
                                     start=True, stop=True)
                last.then_inc(s1_ps, 1)

            def mix1(n, i):
                r = i % 2
                pe.wait_ge(masked1, n + 1)
                pe.wait_ge(v1_sb, n + 1)
                after(pe, y1_sb, n)
                w = E1 + 1
                for h in range(2):
                    p = pT1[:, r, h, :]
                    o = [y_b[:, tt, h * w:(h + 1) * w] for tt in range(TT)]
                    pe.matmul(o[0], p[:, 0:P], v1[:, i % 4, 0, h, :], start=True, stop=True)
                    pe.matmul(o[1], p[:, P:T], v1[:, i % 4, 0, h, :], start=True, stop=False)
                    last = pe.matmul(o[1], p[:, T:T + P], v1[:, i % 4, 1, h, :], start=False, stop=True)
                last.then_inc(y1_ps, 1)

            def transposes_y(n, i):
                pe.wait_ge(y1_sb, n + 1)
                o = tr[0].rearrange("p (h t) -> p h t", h=2)
                for tt in range(TT):
                    for h in range(2):
                        last = pe.transpose(o[:, h, tt * P:(tt + 1) * P], y1[:, i % 2, tt, h, :], ident[:])
                last.then_inc(yT1_ps, 1)

            def project_o(n, i):
                par, r = (i // NB) % 2, i % 2
                pe.wait_ge(yT1l_sb, n + 1)
                w = [v[:, par, 1536:2048].rearrange("p (h d) -> p h d", h=2) for v in (bw_h, bw_l)]
                o = banks[1][:, :].rearrange("p (t d) -> p t d", t=TT)
                for tt in range(TT):
                    c = slice(tt * P, (tt + 1) * P)
                    for h in range(2):
                        pe.matmul(o[:, tt, :], yT1h[:, r, h, c], w[0][:, h, :], start=h == 0, stop=False)
                        pe.matmul(o[:, tt, :], yT1l[:, r, h, c], w[0][:, h, :], start=False, stop=False)
                        last = pe.matmul(o[:, tt, :], yT1h[:, r, h, c], w[1][:, h, :], start=False, stop=h == 1)
                last.then_inc(o1_ps, 1)

            def unit_pair(w, first):
                for i in range(2 * NB):
                    n = 2 * NB * w + i
                    if i % NB == 0:
                        pe.wait_ge(bw_lo, 4 * (2 * w + i // NB + 1))
                    after(pe, v1_sb, n)
                    if first and i == 0:
                        pe.wait_ge(s0_sb, NB)
                    if first and i < NB:
                        pe.wait_ge(xT1_loaded[i], 32)
                    project_qk(n, i, 0)
                    after(pe, acc1, n - 3)
                    if first and i == 1:
                        pe.wait_ge(xT1l_sb, NB)
                    if first and i == 2:
                        pe.wait_ge(rth_sb, NB)
                    if first and i == 5:
                        pe.wait_ge(probT_sb, NB)
                    project_qk(n, i, 1)
                    if not first or i >= 1:
                        if not first or i >= 3:
                            pe.wait_ge(yT1l_sb, n - 2)
                        if first and i == 1:
                            pe.wait_ge(gf_sb, NB)
                        transposes_qk(n - 1, i - 1)
                    pe.wait_ge(xs_sb, 2 * n + 1)
                    project_v(n, i)
                    if not first or i >= 2:
                        mix1(n - 2, i - 2)
                    pe.wait_ge(xs_sb, 2 * n + 2)
                    if first and i == 0:
                        norm_T1(t, 1)
                    if first and i == 1:
                        logits_T(t, 1)
                    if not first or i >= 3:
                        project_o(n - 3, i - 3)
                    if not first or i >= 1:
                        scores1(n - 1, i - 1)
                    if not first or i >= 2:
                        pe.wait_ge(qT1_sb, n)
                        transposes_y(n - 2, i - 2)
                    if first and i == 1:
                        logits(t)
                    if first and i == 4:
                        pe.wait_ge(acc1, 2)
                        route_T(t, 1)

            unit_pair(0, True)
            with pe.Fori(1, NU // 2) as w:
                unit_pair(w, False)
            n = NU * NB
            pe.wait_ge(yT1l_sb, n - 2)
            transposes_qk(n - 1, -1)
            mix1(n - 2, -2)
            pe.wait_ge(acc1, n - 3)
            project_o(n - 3, -3)
            scores1(n - 1, -1)
            pe.wait_ge(qT1_sb, n)
            transposes_y(n - 2, -2)
            pe.wait_ge(acc1, n - 2)
            project_o(n - 2, -2)
            mix1(n - 1, -1)
            pe.wait_ge(yT1l_sb, n - 1)
            transposes_y(n - 1, -1)
            pe.wait_ge(acc1, n - 1)
            project_o(n - 1, -1)

            b1 = [banks[0][:, :], banks[1][:, :]]
            b3 = [trio[:, 0, :], trio[:, 1, :]]
            bp = [trio[:, 2, :], more[:, 0, :]]
            bo = [more[:, 1, :], more[:, 2, :]]

            def hidden_up(m, i):
                par, blk, c, r = (i // 8) % 2, (i % 8) // 2, i % 2, i % 2
                cols = slice(blk * BLK, (blk + 1) * BLK)
                for s, o, read, done in ((0, b1[r], u_sb, up1_ps), (1, b3[r], h3_sb, gate_ps)):
                    w = [v[:, par, 512 * s:512 * s + 512].rearrange("p (k c h) -> p k c h", k=KD, c=2)
                         for v in (cw_h, cw_l)]
                    after(pe, read, m - 1)
                    for k in range(KD):
                        last = three(o, w[0][:, k, c, :], w[1][:, k, c, :], xT1h[:, k, cols], xT1l[:, k, cols],
                                     k == 0, k == KD - 1)
                    last.then_inc(done, 1)

            def spread_probs(m, i):
                par, blk, c, r = (i // 8) % 2, (i % 8) // 2, i % 2, i % 2
                after(pe, wu_sb, m - 1)
                pe.matmul(bp[r], rows_cur[:, par, c, :], probT[:, blk * BLK:(blk + 1) * BLK],
                          start=True, stop=True).then_inc(prob_ps, 1)

            def hidden_down(m, i):
                par, c, r = (i // 8) % 2, i % 2, i % 2
                pe.wait_ge(z1l_sb, m + 1)
                w = [v[:, par, 1024:1536].rearrange("p (c d) -> p c d", c=2) for v in (cw_h, cw_l)]
                if c == 0:
                    after(pe, acc_sb, m)
                for k in range(KD):
                    d = slice(k * P, (k + 1) * P)
                    last = three(bo[k], w[0][:, c, d], w[1][:, c, d], z1h[:, r, :], z1l[:, r, :], c == 0, c == 1)
                last.then_inc(down1_ps, 1)

            def four_chunks(w, first, final):
                for i in range(16):
                    m = 16 * w + i
                    shared = final and i >= 8
                    if i % 8 == 0:
                        pe.wait_ge(cw_lo, 3 * (2 * w + i // 8 + 1))
                        if not shared:
                            pe.wait_ge(rows_made, 2 * w + i // 8 + 1)
                    hidden_up(m, i)
                    if not shared:
                        spread_probs(m, i)
                    if not first or i >= 2:
                        hidden_down(m - 2, i - 2)
                    if final and i in (13, 15):
                        gate_T((i - 13) // 2)

            def gate_T(n):
                pe.wait_ge(go_sb, n + 1)
                for b in (2 * n, 2 * n + 1):
                    if n == 0:
                        pe.wait_ge(wu_sb, 8 * (C_PAIRS - 1))
                    else:
                        pe.wait_ge(so_sb, b - 1)
                    o = bp[b % 2].rearrange("p (t d) -> p t d", t=TT)
                    for t in range(TT):
                        c = (b % 2) * T + t * P
                        for k in range(KD):
                            last = pe.transpose(o[:, t, k * P:(k + 1) * P], g_o[:, k, c:c + P], ident[:])
                    last.then_inc(gT_ps, 1)

            pe.wait_ge(acc1, NU * NB)
            four_chunks(0, True, False)
            with pe.Fori(1, NC // 4 - 1) as w:
                four_chunks(w, False, False)
            four_chunks(NC // 4 - 1, False, True)
            m = 16 * (NC // 4)
            hidden_down(m - 2, -2)
            hidden_down(m - 1, -1)
            gate_T(2)
            gate_T(3)

        @block.scalar
        def _(act):
            raw_ready(act, 0)
            act.activation(wqk_h[:].rearrange("p k c -> p (k c)"), raw[:, 0, 0:KD * NG * P], ACT.Copy).then_inc(wa_hi, 1)

            def norm_T0(b):
                act.wait_ge(xT0_ps, b + 1)
                act.activation(xT0h[:].rearrange("p k t -> p (k t)"), banks[0][:, :], ACT.Copy).then_inc(xT0h_sb, 1)

            def queries_keys(b, pair):
                act.wait_ge(qk0_ps, 2 * b + pair + 1)
                after(act, kT0l_sb, 2 * b + pair)
                act.activation(kT0[0:GR, :, :].rearrange("p g t -> p (g t)"), banks[1][GR:2 * GR, :], ACT.Copy)\
                   .then_inc(kT0_sb, 1)
                after(act, s0_ps, 4 * (b - 1) + 2 * pair + 2)
                act.activation(qT0h[0:GR, 2 * pair:2 * pair + 2, :].rearrange("p g t -> p (g t)"),
                               banks[1][0:GR, :], ACT.Copy).then_inc(qT0h_sb, 1)
                act.wait_ge(kT0_sb, 2 * b + pair + 1)
                act.activation(kT0h[0:GR, 2 * pair:2 * pair + 2, :], kT0[0:GR, :, :], ACT.Copy).then_inc(kT0h_sb, 1)

            def exps(b, g):
                act.wait_ge(max0, 8 * b + 2 * g + 2)
                for t in range(TT):
                    for h in range(GH):
                        c = slice(h * P, (h + 1) * P)
                        if t == 0:
                            o, i = pex[:, 0, h, :], trio[:, 0, c]
                        else:
                            o, i = pex[:, 1:3, h, :], trio[:, 1:3, c]
                        last = act.activation(o, i, ACT.Exp, bias=nmax[:, g, t, h:h + 1])
                last.then_inc(exp0, 1)

            def probs_T(b, g, blocks):
                after(act, y0_ps, 4 * b + g)
                for i in blocks:
                    n = 3 * g + i
                    act.wait_ge(pT0_ps, 12 * b + n + 1)
                    act.activation(pT0[:, i, :, :].rearrange("p h q -> p (h q)"), more[:, n % 2, :], ACT.Copy)\
                       .then_inc(pT0_sb, 1)

            def gate_tanh(b, j):
                n = UP_BANK[j]
                act.wait_ge(up_ps, 8 * b + j + 1)
                after(act, hid_sb, 8 * b + j - 1)
                act.activation(th0[:, j % 2, :], banks[n][:, 0:T], ACT.Tanh, scale=0.5).then_inc(th0_sb, 1)

            def hidden_hi(b, j):
                act.wait_ge(hid_sb, 8 * b + j + 1)
                after(act, down_ps, 8 * b + j - 3)
                act.activation(hid_h[:, j % 4, :], hid[:, j % 2, :], ACT.Copy).then_inc(hidh_sb, 1)

            def gate_out(b):
                act.wait_ge(down_ps, 8 * b + 8)
                after(act, x1_sb, b)
                act.activation(gate0[:].rearrange("p t d -> p (t d)"), more[:, 2, :], ACT.Tanh, scale=0.5)\
                   .then_inc(thf_sb, 1)

            def norm_T1(b, n=0):
                act.wait_ge(xT1_ps, b + 1)
                after(act, xT1_stored, 32 * b)
                after(act, lgT_ps, b)
                act.activation(xT1h_c[:].rearrange("p k t -> p (k t)"), banks[n][:, :], ACT.Copy).then_inc(xT1h_sb, 1)

            def logits_T(b, n=0):
                act.wait_ge(lgT_ps, b + 1)
                act.activation(lgT[:], banks[n][:, 0:T], ACT.Copy).then_inc(lgT_sb, 1)

            def logits_tanh(b):
                act.wait_ge(lg_ps, b + 1)
                o = banks[1][:, 0:TT * P].rearrange("p (t e) -> p t e", t=TT)
                act.activation(r_th[:], o[:, :, 0:NE], ACT.Tanh, scale=0.5).then_inc(rth_sb, 1)

            def route_T(b, n=0):
                act.wait_ge(probT_ps, b + 1)
                act.activation(probT[:, bass.ds(b * T, T)], banks[n][:, 0:T], ACT.Copy).then_inc(probT_sb, 1)

            def project_out(b):
                act.wait_ge(o0_ps, b + 1)
                after(act, x1_sb, b)
                act.activation(s0[:].rearrange("p t d -> p (t d)"), banks[0][:, :], ACT.Copy).then_inc(s0_sb, 1)

            def ffn_hi(n, w):
                raw_ready(act, n)
                act.activation(w[:].rearrange("p k c -> p (k c)"), raw[:, n % 2, :], ACT.Copy).then_inc(wa_hi, 1)

            def batch(b, first, final):
                t = b - 1
                if not first:
                    gate_out(t)
                queries_keys(b, 0)
                if not first:
                    project_out(t)
                if first:
                    act.wait_ge(consts_loaded, 16 * N_CONST)
                    act.activation(qT0h[GR:KR, :, :].rearrange("p g t -> p (g t)"), alibi_q, ACT.Copy)\
                       .then_inc(alibi_hi, 1)
                    act.activation(kz0h[GR:KR, :, :, :].rearrange("p g h t -> p (g h t)"),
                                   alibi_k, ACT.Copy).then_inc(alibi_hi, 1)
                queries_keys(b, 1)
                if first:
                    ffn_hi(2, w1_h)
                act.wait_ge(v0_ps, b + 1)
                after(act, y0_ps, 4 * b)
                act.activation(v0[:, :, :, 0:E0], banks[0][:, :].rearrange("p (t h e) -> p t h e", t=TT, h=H0),
                               ACT.Copy).then_inc(v0_sb, 1)
                if first:
                    ffn_hi(3, w3_h)
                gate_tanh(b, 0)
                exps(b, 0)
                gate_tanh(b, 1)
                hidden_hi(b, 0)
                hidden_hi(b, 1)
                gate_tanh(b, 2)
                probs_T(b, 0, (0, 1))
                gate_tanh(b, 3)
                probs_T(b, 0, (2,))
                if not first:
                    norm_T1(t)
                exps(b, 1)
                if first:
                    act.wait_ge(fw_step, 6)
                    act.activation(w2_h[:].rearrange("p j d -> p (j d)"), raw[:, 1, :], ACT.Copy).then_inc(fw_hi, 1)
                hidden_hi(b, 2)
                hidden_hi(b, 3)
                gate_tanh(b, 4)
                if first:
                    for i in range(4):
                        act.wait_ge(fw_done, i + 1)
                        act.activation(w2_h[:, 2 * i:2 * i + 2, :].rearrange("p j d -> p (j d)"), banks[i % 2][:, :],
                                       ACT.Copy, scale=0.5 * float(FF) ** -0.5).then_inc(w2_hi, 1)
                if not first:
                    logits_T(t)
                hidden_hi(b, 4)
                probs_T(b, 1, (0, 1))
                gate_tanh(b, 5)
                probs_T(b, 1, (2,))
                exps(b, 2)
                hidden_hi(b, 5)
                if not first:
                    logits_tanh(t)
                probs_T(b, 2, (0, 1))
                gate_tanh(b, 6)
                probs_T(b, 2, (2,))
                exps(b, 3)
                hidden_hi(b, 6)
                if not first:
                    route_T(t)
                probs_T(b, 3, (0, 1))
                gate_tanh(b, 7)
                probs_T(b, 3, (2,))
                if not final:
                    norm_T0(b + 1)
                hidden_hi(b, 7)
                act.wait_ge(yT0_ps, b + 1)
                act.activation(yT0h[:].rearrange("p k t -> p (k t)"), banks[0][:, :], ACT.Copy).then_inc(yT0h_sb, 1)

            norm_T0(0)
            raw_ready(act, 1)
            act.activation(wvo_h[:], raw[:, 1, 0:1280], ACT.Copy).then_inc(wa_hi, 1)
            batch(0, True, False)
            with act.Fori(1, NB - 1) as b:
                batch(b, False, False)
            batch(NB - 1, False, True)
            t = NB - 1
            gate_out(t)

            def unit_hi(v, par, q):
                raw_half = (A_LOADS + par) % 2
                if q == 0:
                    act.wait_ge(raw_loaded[raw_half], (v - par) * 8 + 16 * ((A_LOADS + par) // 2 + 1))
                    after(act, o1_ps, NB * (v - 1))
                c = slice(512 * q, 512 * q + 512)
                act.activation(bw_h[:, par, c], raw[:, raw_half, c], ACT.Copy).then_inc(bw_hi, 1)

            def scores_exp(n, i):
                r = i % 2
                act.wait_ge(s1_ps, n + 1)
                act.wait_ge(rstd_sb, n + 1)
                for h in range(2):
                    act.activation(pT1[:, r, h, 0:T], trio[:, 0, h * T:(h + 1) * T], ACT.Tanh,
                                   scale=rstd[:, r, 2 + h:3 + h])
                    last = act.activation(pT1[:, r, h, T:T + P], trio[:, 1, h * P:(h + 1) * P], ACT.Tanh,
                                          scale=rstd[:, r, 6 + h:7 + h])
                last.then_inc(tanh1, 1)

            def step(n, i, first, last_unit, next_unit):
                def live(lag):
                    return not first or i >= lag
                for tt in range(TT):
                    act.wait_ge(qk1_ps, 2 * n + tt + 1)
                    if tt == 0:
                        after(act, qT1_ps, n - 1)
                    act.activation(xs[:, i % 2, tt, :, :, :].rearrange("p s h e -> p (s h e)"), banks[tt][:, :],
                                   ACT.Copy).then_inc(xs_sb, 1)
                    if first and i == 5 and tt == 0:
                        route_T(t, 1)
                act.wait_ge(v1_ps, n + 1)
                if first and i == 0:
                    act.wait_ge(v1_ones, 1)
                act.activation(v1[:, i % 4, :, :, 0:E1], banks[0][:, :].rearrange("p (t h e) -> p t h e", t=TT, h=2),
                               ACT.Copy).then_inc(v1_sb, 1)
                if first and i == 0:
                    norm_T1(t, 1)
                if live(1):
                    key_query(n - 1, i - 1)
                    if first and i == 1:
                        logits_T(t, 1)
                    scores_exp(n - 1, i - 1)
                    if first and i == 1:
                        logits_tanh(t)
                if first and i == 2:
                    act.wait_ge(xT1_stored, 32 * NB)
                if live(2):
                    out_hi(n - 2, i - 2)
                if live(1):
                    numerators(n - 1, i - 1)
                if not last_unit and 3 <= i % NB < 7:
                    unit_hi(next_unit, (i // NB + 1) % 2, i % NB - 3)

            def key_query(n, i):
                act.wait_ge(qT1_ps, n + 1)
                act.activation(qT1[:, i % 2, :, :].rearrange("p h t -> p (h t)"), trio[:, 2, :], ACT.Copy)\
                   .then_inc(qT1_sb, 1)

            def numerators(n, i):
                act.wait_ge(tanh1, n + 1)
                p = pT1[:, i % 2, :, :].rearrange("p h t -> p (h t)")
                act.activation(p, p, ACT.Exp, scale=CAP).then_inc(exp1, 1)

            def out_hi(n, i):
                act.wait_ge(yT1_ps, n + 1)
                after(act, o1_ps, n - 1)
                act.activation(yT1h[:, i % 2, :, :].rearrange("p h t -> p (h t)"), trio[:, 2, :], ACT.Copy)\
                   .then_inc(yT1h_sb, 1)

            def unit_pair(w, first, final):
                for i in range(2 * NB):
                    step(2 * NB * w + i, i, first, final and i >= NB, 2 * w + i // NB + 1)

            for q in range(4):
                unit_hi(0, 0, q)
            project_out(t)
            unit_pair(0, True, False)
            with act.Fori(1, NU // 2 - 1) as w:
                unit_pair(w, False, False)
            unit_pair(NU // 2 - 1, False, True)
            def pair_hi(p, par, q):
                raw_half = (A_LOADS + NU + par) % 2
                if q == 0:
                    act.wait_ge(raw_loaded[raw_half], (p - par) * 8 + 16 * ((A_LOADS + NU + par) // 2 + 1))
                    after(act, down1_ps, 8 * (p - 1))
                c = slice(512 * q, 512 * q + 512)
                act.activation(cw_h[:, par, c], raw[:, raw_half, c], ACT.Copy).then_inc(cw_hi, 1)

            def pair_rows(p, par):
                act.activation(rows_cur[:, par, :, :].rearrange("p c h -> p (c h)"),
                               raw[:, (A_LOADS + NU + par) % 2, 1536:1536 + 2 * P], ACT.Copy).then_inc(rows_made, 1)

            n = NU * NB
            key_query(n - 1, -1)
            scores_exp(n - 1, -1)
            out_hi(n - 2, -2)
            numerators(n - 1, -1)
            for q in range(3):
                pair_hi(0, 0, q)
            pair_rows(0, 0)
            out_hi(n - 1, -1)

            def expert_step(m, i, shared):
                r = i % 2
                act.wait_ge(gate_ps, m + 1)
                after(act, z1_sb, m - 1)
                act.activation(h3[:, r, :], trio[:, r, :], ACT.Copy).then_inc(h3_sb, 1)
                if shared:
                    act.wait_ge(up1_ps, m + 1)
                    act.activation(th1[:, r, :], banks[r][:, :], ACT.Tanh, scale=0.5).then_inc(th1_sb, 1)
                else:
                    act.wait_ge(u_sb, m + 1)
                    act.activation(th1[:, r, :], u[:, r, :], ACT.Tanh, scale=0.5).then_inc(th1_sb, 1)
                act.wait_ge(z1_sb, m + 1)
                after(act, down1_ps, m - 1)
                act.activation(z1h[:, r, :], z1[:, r, :], ACT.Copy).then_inc(z1h_sb, 1)

            def four_chunks(w, final):
                for i in range(16):
                    expert_step(16 * w + i, i, final and i >= 8)
                    if 3 <= i % 8 < 6 and not (final and i >= 8):
                        p, par = 2 * w + i // 8 + 1, (i // 8 + 1) % 2
                        pair_hi(p, par, i % 8 - 3)
                        if i % 8 == 3 and not final:
                            pair_rows(p, par)
                    if final and i in (11, 13, 15):
                        gate_tanh_out((i - 11) // 2)

            def gate_tanh_out(n):
                act.wait_ge(acc_sb, 8 * (C_PAIRS - 1) + 2 * n + 2)
                after(act, go_sb, n)
                act.activation(th_o[:], acc[:, :, n * BLK:(n + 1) * BLK], ACT.Tanh, scale=0.25).then_inc(tho_sb, 1)

            act.wait_ge(acc1, NU * NB)
            four_chunks(0, False)
            with act.Fori(1, NC // 4 - 1) as w:
                four_chunks(w, False)
            four_chunks(NC // 4 - 1, True)
            gate_tanh_out(3)

        @block.vector
        def _(dve):
            def tile(b, t):
                return xs_all[:, bass.ds(2 * b + t, 1), :].rearrange("p a d -> p (a d)")

            def seq(b):
                return xs_all[:, bass.ds(2 * b, TT), :]

            def f32(ap):
                return ap.bitcast(F32)

            def lo(out, full, hi):
                return dve.tensor_tensor(out=out, in0=full, in1=f32(hi), op=ALU.subtract)

            def stats(b, st, mv, ve, st_sem, mv_sem, ve_sem, x1_ready=None):
                if isinstance(b, int) and b == 0:
                    dve.wait_ge(x0_loaded, 16)
                else:
                    dve.wait_ge(x_loaded, 32)
                if x1_ready is not None:
                    dve.wait_ge(x1_sb, x1_ready)
                    dve.tensor_copy(waited[:], ident[:, 0:1])
                for t in range(TT):
                    last = dve.bn_stats(out=st[:, t, :], in_=tile(b, t))
                last.then_inc(st_sem, 1)
                dve.wait_ge(st_sem, b + 1)
                dve.tensor_copy(waited[:], st[:, 0, 0:1])
                for t in range(TT):
                    last = dve.bn_aggr(out=mv[:, t, :], in_=st[:, t, :])
                last.then_inc(mv_sem, 1)
                dve.wait_ge(mv_sem, b + 1)
                dve.tensor_scalar(out=ve[:], in0=mv[:, :, 1], scalar1=LN_EPS, scalar2=None, op0=ALU.add)\
                   .then_inc(ve_sem, 1)

            def normalise(b, xn, mv, rs, rs_sem, xn_sem):
                dve.wait_ge(rs_sem, b + 1)
                for t in range(TT):
                    dve.tensor_scalar(out=xn[:, t, :], in0=tile(b, t), scalar1=mv[:, t, 0:1], scalar2=rs[:, t:t + 1],
                                      op0=ALU.subtract, op1=ALU.mult).then_inc(xn_sem, 1)

            stats(0, st0, mv0, ve0, st0_sb, mv0_sb, ve0_sb)
            normalise(0, xn0, mv0, rs0, rs0_sb, xn0_sb)
            raw_ready(dve, 0)
            dve.wait_ge(wa_hi, 1)
            lo(wqk_l[:].rearrange("p k c -> p (k c)"), raw[:, 0, 0:KD * NG * P], wqk_h[:].rearrange("p k c -> p (k c)"))\
                .then_inc(wa_lo, 1)

            def norm_T0(b):
                dve.wait_ge(xT0h_sb, b + 1)
                lo(xT0l[:].rearrange("p k t -> p (k t)"), banks[0][:, :], xT0h[:].rearrange("p k t -> p (k t)"))\
                    .then_inc(xT0l_sb, 1)

            def keys_lo(b, pair):
                dve.wait_ge(kT0h_sb, 2 * b + pair + 1)
                c = slice(2 * pair, 2 * pair + 2)
                lo(kT0l[0:GR, c, :], kT0[0:GR, :, :], kT0h[0:GR, c, :]).then_inc(kT0l_sb, 1)

            def first_head_keys(b):
                dve.wait_ge(kT0h_sb, 2 * b + 1)
                after(dve, s0_ps, 4 * b - 1)
                dve.tensor_tensor(out=kz0h[0:GR, 0, :, :], in0=f32(kT0h[0:GR, 0, :]).unsqueeze(1).to_broadcast([GR, GH, T]),
                                  in1=head_mask[0:GR, :].unsqueeze(2).to_broadcast([GR, GH, T]), op=ALU.mult)\
                   .then_inc(kz0h_sb, 1)

            def queries_lo(b, pair):
                dve.wait_ge(qT0h_sb, 2 * b + pair + 1)
                lo(qT0l[0:GR, 2 * pair:2 * pair + 2, :].rearrange("p g t -> p (g t)"), banks[1][0:GR, :],
                   qT0h[0:GR, 2 * pair:2 * pair + 2, :].rearrange("p g t -> p (g t)")).then_inc(qT0l_sb, 1)

            def maxima(b, g):
                dve.wait_ge(s0_ps, 4 * b + g + 1)
                dve.tensor_reduce(out=nmax[:, g, 0, :], in_=trio[:, 0, :].rearrange("p (h k) -> p h k", h=GH),
                                  axis=AX.X, op=ALU.max, negate=True).then_inc(max0, 1)
                dve.tensor_reduce(out=nmax[:, g, 1, :], in_=trio[:, 1:3, :].rearrange("p c (h k) -> p h c k", h=GH),
                                  axis=AX.XY, op=ALU.max, negate=True).then_inc(max0, 1)

            def hidden(b, j):
                n = UP_BANK[j]
                r = j % 2
                dve.wait_ge(th0_sb, 8 * b + j + 1)
                dve.scalar_tensor_tensor(out=th0[:, r, :], in0=th0[:, r, :], scalar=1.0, in1=banks[n][:, 0:T],
                                         op0=ALU.add, op1=ALU.mult).then_inc(z0_sb, 1)
                dve.wait_ge(z0_sb, 8 * b + j + 1)
                after(dve, hidl_sb, 8 * b + j - 1)
                dve.tensor_tensor(out=hid[:, r, :], in0=banks[n][:, T:2 * T], in1=th0[:, r, :], op=ALU.mult)\
                   .then_inc(hid_sb, 1)

            def heads_out(b, g):
                n = MIX_BANK[g]
                dve.wait_ge(y0_ps, 4 * b + g + 1)
                o = banks[n][:, 0:TT * GH * (E0 + 1)].rearrange("p (t h e) -> p t h e", t=TT, h=GH)
                dve.reciprocal(out=rden0[:, g, :, :], in_=o[:, :, :, E0]).then_inc(rden0_sb, 1)
                dve.wait_ge(rden0_sb, 4 * b + g + 1)
                y = y0[:, :, g * GH * E0:(g + 1) * GH * E0].rearrange("p t (h e) -> p t h e", h=GH)
                dve.tensor_tensor(out=y, in0=o[:, :, :, 0:E0],
                                  in1=rden0[:, g, :, :].unsqueeze(3).to_broadcast([P, TT, GH, E0]), op=ALU.mult)\
                   .then_inc(y0_sb, 1)

            def gate_out(b):
                dve.wait_ge(thf_sb, b + 1)
                flat = gate0[:].rearrange("p t d -> p (t d)")
                dve.scalar_tensor_tensor(out=flat, in0=flat, scalar=1.0, in1=more[:, 2, :], op0=ALU.add, op1=ALU.mult)\
                   .then_inc(gf_sb, 1)

            def gate_s(b):
                dve.wait_ge(gf_sb, b + 1)
                dve.wait_ge(s0_sb, b + 1)
                dve.tensor_tensor(out=gate0[:], in0=gate0[:], in1=s0[:], op=ALU.mult).then_inc(sgf_sb, 1)

            def residual(b):
                dve.wait_ge(sgf_sb, b + 1)
                dve.scalar_tensor_tensor(out=seq(b), in0=gate0[:], scalar=0.5, in1=seq(b), op0=ALU.mult, op1=ALU.add)\
                   .then_inc(x1_sb, 1)

            def norm_T1(b, n=0):
                dve.wait_ge(xT1h_sb, b + 1)
                lo(xT1l_c[:].rearrange("p k t -> p (k t)"), banks[n][:, :], xT1h_c[:].rearrange("p k t -> p (k t)"))\
                    .then_inc(xT1l_sb, 1)

            def router(b, parts=(0, 1)):
                n = [5 * parts[0]]

                def link(ins):
                    n[0] += 1
                    ins.then_inc(route, 1)
                    dve.wait_ge(route, 10 * b + n[0])

                four = [P, TT, NE, NE]
                if 0 in parts:
                    dve.wait_ge(rth_sb, b + 1)
                    link(dve.scalar_tensor_tensor(out=r_sc[:], in0=r_th[:], scalar=0.5,
                                                  in1=gate_bias[:].unsqueeze(1).to_broadcast([P, TT, NE]),
                                                  op0=ALU.mult, op1=ALU.add))
                    other, own = r_sc[:].unsqueeze(2).to_broadcast(four), r_sc[:].unsqueeze(3).to_broadcast(four)
                    link(dve.tensor_tensor(out=r_ge[:], in0=other, in1=own, op=ALU.is_ge))
                    link(dve.tensor_tensor(out=r_ge[:], in0=r_ge[:], in1=before[:].unsqueeze(1).to_broadcast(four),
                                           op=ALU.mult))
                    link(dve.tensor_tensor(out=r_gt[:], in0=other, in1=own, op=ALU.is_gt))
                    link(dve.tensor_tensor(out=r_gt[:], in0=r_gt[:], in1=r_ge[:], op=ALU.max))
                if 1 in parts:
                    link(dve.tensor_reduce(out=r_rank[:], in_=r_gt[:], axis=AX.X, op=ALU.add))
                    link(dve.scalar_tensor_tensor(out=r_w[:], in0=r_rank[:], scalar=float(TOPK), in1=r_sc[:],
                                                  op0=ALU.is_lt, op1=ALU.mult))
                    link(dve.tensor_reduce(out=r_sum[:], in_=r_w[:], axis=AX.X, op=ALU.add))
                    link(dve.reciprocal(out=r_sum[:], in_=r_sum[:]))
                    link(dve.tensor_tensor(out=r_p[:], in0=r_w[:], in1=r_sum[:].unsqueeze(2).to_broadcast([P, TT, NE]),
                                           op=ALU.mult))
                    after(dve, probT_ps, b)
                    dve.tensor_copy(r_split[:, :, 0:NE], r_p[:]).then_inc(split_hi, 1)
                    dve.wait_ge(split_hi, b + 1)
                    lo(r_split[:, :, NE:2 * NE], r_p[:], r_split[:, :, 0:NE]).then_inc(split_sb, 1)

            def butterfly(k):
                s = 1 << k // 2
                dve.wait_ge(w2_loaded, 16)
                after(dve, fw_step, 2 * (k // 2))
                dve.wait_ge(wa_lo, 4)
                w2_b = xs_all[:, NT // 2:NT, :].rearrange("p t d -> p (t d)")
                places = [w2_a[:], w2_b, w2_a[:], raw[:, 1, :]]
                i, o = [v.rearrange("p (g two c) -> p g two c", two=2, c=s * D) for v in places[k // 2:k // 2 + 2]]
                dve.tensor_tensor(out=o[:, :, k % 2, :], in0=i[:, :, 0, :], in1=i[:, :, 1, :],
                                  op=(ALU.add, ALU.subtract)[k % 2]).then_inc(fw_step, 1)

            def hadamard_lo():
                dve.wait_ge(fw_hi, 1)
                lo(w2_l[:].rearrange("p j d -> p (j d)"), raw[:, 1, :], w2_h[:].rearrange("p j d -> p (j d)"))\
                    .then_inc(fw_lo, 1)
                for i in range(4):
                    dve.wait_ge(w2_hi, i + 1)
                    c = slice(2 * i, 2 * i + 2)
                    dve.scalar_tensor_tensor(out=w2_l[:, c, :].rearrange("p j d -> p (j d)"), in0=banks[i % 2][:, :],
                                             scalar=0.5 * float(FF) ** -0.5,
                                             in1=f32(w2_h[:, c, :]).rearrange("p j d -> p (j d)"),
                                             op0=ALU.mult, op1=ALU.subtract).then_inc(w2_lo, 1)

            def batch(b, first, final):
                t = b - 1
                def beside(*steps):
                    for k in steps if first else ():
                        butterfly(k)

                def ffn_lo(n, wl, wh):
                    dve.wait_ge(wa_hi, n + 1)
                    lo(wl[:].rearrange("p k c -> p (k c)"), raw[:, n % 2, :], wh[:].rearrange("p k c -> p (k c)"))\
                        .then_inc(wa_lo, 1)

                queries_lo(b, 0)
                keys_lo(b, 0)
                first_head_keys(b)
                if not first:
                    gate_out(t)
                if first:
                    dve.wait_ge(alibi_hi, 2)
                    lo(qT0l[GR:KR, :, :].rearrange("p g t -> p (g t)"), alibi_q,
                       qT0h[GR:KR, :, :].rearrange("p g t -> p (g t)")).then_inc(alibi_lo, 1)
                    lo(kz0l[GR:KR, :, :, :].rearrange("p g h t -> p (g h t)"),
                       alibi_k,
                       kz0h[GR:KR, :, :, :].rearrange("p g h t -> p (g h t)")).then_inc(alibi_lo, 1)
                queries_lo(b, 1)
                keys_lo(b, 1)
                if first:
                    ffn_lo(2, w1_l, w1_h)
                    ffn_lo(3, w3_l, w3_h)
                maxima(b, 0)
                if not first:
                    gate_s(t)
                beside(0)
                hidden(b, 0)
                if not first:
                    residual(t)
                beside(1)
                hidden(b, 1)
                beside(2)
                if not first:
                    stats(t, st1, mv1, ve1, st1_sb, mv1_sb, ve1_sb, b)
                hidden(b, 2)
                beside(3, 4)
                if not first:
                    normalise(t, xn1, mv1, rs1, rs1_sb, xn1_sb)
                maxima(b, 1)
                beside(5)
                hidden(b, 3)
                if not first:
                    norm_T1(t)
                heads_out(b, 0)
                hidden(b, 4)
                if first:
                    hadamard_lo()
                maxima(b, 2)
                if not final:
                    stats(b + 1, st0, mv0, ve0, st0_sb, mv0_sb, ve0_sb)
                hidden(b, 5)
                heads_out(b, 1)
                if not first:
                    router(t)
                maxima(b, 3)
                hidden(b, 6)
                heads_out(b, 2)
                if not final:
                    normalise(b + 1, xn0, mv0, rs0, rs0_sb, xn0_sb)
                hidden(b, 7)
                if not final:
                    norm_T0(b + 1)
                heads_out(b, 3)
                dve.wait_ge(yT0h_sb, b + 1)
                lo(yT0l[:].rearrange("p k t -> p (k t)"), banks[0][:, :], yT0h[:].rearrange("p k t -> p (k t)"))\
                    .then_inc(yT0l_sb, 1)

            norm_T0(0)
            raw_ready(dve, 1)
            dve.wait_ge(wa_hi, 2)
            lo(wvo_l[:], raw[:, 1, 0:1280], wvo_h[:]).then_inc(wa_lo, 1)
            dve.wait_ge(consts_loaded, 16 * N_CONST)
            dve.tensor_copy(ident_b[:], ident[:])
            dve.tensor_copy(tri_add[:], tri_add32[:].unsqueeze(1).to_broadcast([P, GH, P]))
            dve.tensor_copy(hadamard_r[:], hadamard[:])
            dve.tensor_scalar(out=gate_bias[:], in0=gate_bias[:], scalar1=0.5, scalar2=None, op0=ALU.add)\
               .then_inc(consts_made, 1)
            batch(0, True, False)
            with dve.Fori(1, NB - 1) as b:
                batch(b, False, False)
            batch(NB - 1, False, True)
            t = NB - 1
            gate_out(t)

            def unit_lo(v, par, q):
                half = (A_LOADS + par) % 2
                dve.wait_ge(bw_hi, 4 * v + q + 1)
                c = slice(512 * q, 512 * q + 512)
                lo(bw_l[:, par, c], raw[:, half, c], bw_h[:, par, c]).then_inc(bw_lo, 1)

            def squares(n, i, tt):
                dve.wait_ge(xs_sb, 2 * n + tt + 1)
                x_qk = xs[:, i % 2, tt, :, :, :].rearrange("p s h e -> p (s h e)")
                dve.tensor_tensor(out=sq[:, tt, :], in0=x_qk, in1=x_qk, op=ALU.mult).then_inc(sq_sb, 1)
                dve.wait_ge(sq_sb, 2 * n + tt + 1)
                dve.tensor_reduce(out=ssq[:, i % 2, tt, :], in_=sq[:, tt, :].rearrange("p (h e) -> p h e", h=4),
                                  axis=AX.X, op=ALU.add).then_inc(ssq_sb, 1)

            def mean_squares(n, i):
                dve.wait_ge(ssq_sb, 2 * n + 2)
                dve.tensor_scalar(out=msq[:, i % 2, :], in0=ssq[:, i % 2, :, :].rearrange("p t h -> p (t h)"),
                                  scalar1=1.0 / E1, scalar2=RMS_EPS, op0=ALU.mult, op1=ALU.add).then_inc(msq_sb, 1)

            def key_T(n, i, unit):
                dve.wait_ge(kT1_ps, n + 1)
                dve.tensor_tensor(out=kT1[:, i % 2, :, :], in0=more[:, 2, :].rearrange("p (h t) -> p h t", h=2),
                                  in1=qk_scale[:, bass.ds(2 * unit, 2)].unsqueeze(2).to_broadcast([P, 2, T]),
                                  op=ALU.mult).then_inc(kT1_sb, 1)

            def heads_out1(n, i):
                dve.wait_ge(y1_ps, n + 1)
                o = more[:, 0:2, 0:2 * (E1 + 1)].rearrange("p t (h e) -> p t h e", h=2)
                dve.reciprocal(out=rden1[:, i % 2, :, :], in_=o[:, :, :, E1]).then_inc(rden1_sb, 1)
                dve.wait_ge(rden1_sb, n + 1)
                dve.tensor_tensor(out=y1[:, i % 2, :, :, :], in0=o[:, :, :, 0:E1],
                                  in1=rden1[:, i % 2, :, :].unsqueeze(3).to_broadcast([P, TT, 2, E1]), op=ALU.mult)\
                   .then_inc(y1_sb, 1)

            def add_unit(n, i, first):
                b = i % NB
                dve.wait_ge(o1_ps, n + 1)
                s = s_acc[:, 2 * b:2 * b + 2, :].rearrange("p t d -> p (t d)")
                if first and 0 <= i < NB:
                    dve.tensor_copy(s, banks[1][:, :]).then_inc(acc1, 1)
                else:
                    after(dve, acc1, n + 1 - NB)
                    dve.tensor_tensor(out=s, in0=banks[1][:, :], in1=s, op=ALU.add).then_inc(acc1, 1)

            def out_lo(n, i):
                dve.wait_ge(yT1h_sb, n + 1)
                lo(yT1l[:, i % 2, :, :].rearrange("p h t -> p (h t)"), trio[:, 2, :],
                   yT1h[:, i % 2, :, :].rearrange("p h t -> p (h t)")).then_inc(yT1l_sb, 1)

            def unit_pair(w, first, final):
                for i in range(2 * NB):
                    n = 2 * NB * w + i

                    def live(lag):
                        return not first or i >= lag
                    squares(n, i, 0)
                    squares(n, i, 1)
                    mean_squares(n, i)
                    if first and i == 0:
                        norm_T1(t, 1)
                    if live(1):
                        key_T(n - 1, i - 1, 2 * w + (i - 1) // NB)
                    if live(2):
                        heads_out1(n - 2, i - 2)
                    if live(3):
                        add_unit(n - 3, i - 3, first)
                    if live(2):
                        out_lo(n - 2, i - 2)
                    if first and i in (2, 3):
                        router(t, (i - 2,))
                    if 3 <= i % NB < 7 and not (final and i >= NB):
                        unit_lo(2 * w + i // NB + 1, (i // NB + 1) % 2, i % NB - 3)

            dve.wait_ge(yT0_ps, NB)
            for q in range(4):
                unit_lo(0, 0, q)
            gate_s(t)
            residual(t)
            stats(t, st1, mv1, ve1, st1_sb, mv1_sb, ve1_sb, NB)
            normalise(t, xn1, mv1, rs1, rs1_sb, xn1_sb)
            dve.wait_ge(rope_made, 6)
            unit_pair(0, True, False)
            with dve.Fori(1, NU // 2 - 1) as w:
                unit_pair(w, False, False)
            unit_pair(NU // 2 - 1, False, True)
            def pair_lo(p, par, q):
                half = (A_LOADS + NU + par) % 2
                dve.wait_ge(cw_hi, 3 * p + q + 1)
                c = slice(512 * q, 512 * q + 512)
                lo(cw_l[:, par, c], raw[:, half, c], cw_h[:, par, c]).then_inc(cw_lo, 1)

            n = NU * NB
            key_T(n - 1, -1, NU - 1)
            heads_out1(n - 2, -2)
            add_unit(n - 3, -3, False)
            out_lo(n - 2, -2)
            add_unit(n - 2, -2, False)
            for q in range(3):
                pair_lo(0, 0, q)
            heads_out1(n - 1, -1)
            out_lo(n - 1, -1)
            add_unit(n - 1, -1, False)

            def add_pair(m, i, first, halves=range(KD)):
                blk = (i % 8) // 2
                dve.wait_ge(down1_ps, m + 1)
                for k in halves:
                    a = acc[:, k, blk * BLK:(blk + 1) * BLK]
                    if first and 0 <= i < 8:
                        dve.tensor_copy(a, more[:, 1 + k, :]).then_inc(acc_sb, 1)
                    else:
                        dve.wait_ge(acc_sb, m - 7)
                        dve.tensor_tensor(out=a, in0=more[:, 1 + k, :], in1=a, op=ALU.add).then_inc(acc_sb, 1)

            def four_chunks(w, first, final):
                for i in range(16):
                    m, r = 16 * w + i, i % 2
                    shared = final and i >= 8
                    if shared:
                        dve.wait_ge(th1_sb, m + 1)
                        dve.scalar_tensor_tensor(out=u[:, r, :], in0=th1[:, r, :], scalar=1.0, in1=banks[r][:, :],
                                                 op0=ALU.add, op1=ALU.mult).then_inc(u_sb, 1)
                    else:
                        dve.wait_ge(up1_ps, m + 1)
                        dve.wait_ge(h3_sb, m + 1)
                        dve.tensor_tensor(out=u[:, r, :], in0=banks[r][:, :], in1=h3[:, r, :], op=ALU.mult)\
                           .then_inc(u_sb, 1)
                        dve.wait_ge(prob_ps, m + 1)
                        dve.wait_ge(u_sb, m + 1)
                        prob = trio[:, 2, :] if r == 0 else more[:, 0, :]
                        dve.tensor_tensor(out=w_u[:, r, :], in0=prob, in1=u[:, r, :], op=ALU.mult).then_inc(wu_sb, 1)
                    if i % 2 == 1 and (not first or i >= 3):
                        add_pair(m - 2, i - 2, first, (0,))
                    after(dve, z1l_sb, m - 1)
                    if shared:
                        dve.wait_ge(u_sb, m + 1)
                        dve.wait_ge(h3_sb, m + 1)
                        dve.tensor_tensor(out=z1[:, r, :], in0=u[:, r, :], in1=h3[:, r, :], op=ALU.mult)\
                           .then_inc(z1_sb, 1)
                    else:
                        dve.wait_ge(wu_sb, m + 1)
                        dve.wait_ge(th1_sb, m + 1)
                        dve.scalar_tensor_tensor(out=z1[:, r, :], in0=th1[:, r, :], scalar=1.0, in1=w_u[:, r, :],
                                                 op0=ALU.add, op1=ALU.mult).then_inc(z1_sb, 1)
                    if i % 2 == 1 and (not first or i >= 3):
                        add_pair(m - 2, i - 2, first, (1,))
                    if 4 <= i % 8 < 7 and not shared:
                        pair_lo(2 * w + i // 8 + 1, (i // 8 + 1) % 2, i % 8 - 4)
                    if final and i in (12, 14):
                        gate_out1((i - 12) // 2)
                    if final and i == 14:
                        block_out(0)

            def gate_out1(n):
                dve.wait_ge(tho_sb, n + 1)
                after(dve, gT_ps, 2 * n)
                dve.scalar_tensor_tensor(out=g_o[:], in0=th_o[:], scalar=1.0, in1=acc[:, :, n * BLK:(n + 1) * BLK],
                                         op0=ALU.add, op1=ALU.mult).then_inc(go_sb, 1)

            def block_out(n):
                for b in (2 * n, 2 * n + 1):
                    dve.wait_ge(gT_ps, b + 1)
                    gate = trio[:, 2, :] if b % 2 == 0 else more[:, 0, :]
                    s = s_acc[:, 2 * b:2 * b + 2, :].rearrange("p t d -> p (t d)")
                    dve.tensor_tensor(out=s, in0=gate, in1=s, op=ALU.mult).then_inc(so_sb, 1)
                    dve.wait_ge(so_sb, b + 1)
                    xb = xs_all[:, 2 * b:2 * b + 2, :].rearrange("p t d -> p (t d)")
                    dve.scalar_tensor_tensor(out=xb, in0=s, scalar=0.25, in1=xb, op0=ALU.mult, op1=ALU.add)\
                       .then_inc(o_sb_made, 1)

            four_chunks(0, True, False)
            with dve.Fori(1, NC // 4 - 1) as w:
                four_chunks(w, False, False)
            four_chunks(NC // 4 - 1, False, True)
            gate_out1(2)
            block_out(1)
            add_pair(16 * (NC // 4) - 1, -1, False)
            gate_out1(3)
            block_out(2)
            block_out(3)

        @block.gpsimd
        def _(pool):
            pool.memset(half_pow[:], -0.5).then_inc(pow_made, 1)
            pool.memset(v0[:, :, :, E0:E0 + 1], 1.0).then_inc(pow_made, 1)
            pool.memset(r_split[:].bitcast(F32).rearrange("p t e -> p (t e)"), 0.0).then_inc(pow_made, 1)

            def inverse_root(b, ve, rs, ve_sem, rs_sem):
                pool.wait_ge(ve_sem, b + 1)
                pool.tensor_tensor(out=rs[:], in0=ve[:], in1=half_pow[:, 0:TT], op=ALU.pow).then_inc(rs_sem, 1)

            pool.wait_ge(pow_made, 3)
            inverse_root(0, ve0, rs0, ve0_sb, rs0_sb)
            pool.wait_ge(consts_loaded, 16 * N_CONST)

            def head_keys(b, g, parts, before):
                pool.wait_ge(kT0l_sb, 2 * b + g // 2 + 1)
                after(pool, s0_ps, 4 * b + g - 1)
                after(pool, hidl_sb, before)
                for out, k in parts:
                    last = pool.tensor_tensor(out=out[0:GR, g % 2, :, :],
                                              in0=k[0:GR, g, :].bitcast(F32).unsqueeze(1).to_broadcast([GR, GH, T]),
                                              in1=head_mask[0:GR, :].unsqueeze(2).to_broadcast([GR, GH, T]), op=ALU.mult)
                last.then_inc(kz0l_sb, 1)
                pool.wait_ge(kz0l_sb, 4 * b + g + 1)

            def hidden_lo(b, j):
                pool.wait_ge(hidh_sb, 8 * b + j + 1)
                pool.tensor_tensor(out=hid_l[:, j % 4, :], in0=hid[:, j % 2, :], in1=hid_h[:, j % 4, :].bitcast(F32),
                                   op=ALU.subtract).then_inc(hidl_sb, 1)

            def batch(b, first, final):
                t = b - 1
                if not first:
                    pool.wait_ge(rs0_sb, b + 1)
                hi_part, lo_part = (kz0h, kT0h), (kz0l, kT0l)
                head_keys(b, 0, (lo_part,), NJ * b)
                head_keys(b, 1, (hi_part, lo_part), NJ * b)
                hidden_lo(b, 0)
                hidden_lo(b, 1)
                if not first:
                    inverse_root(t, ve1, rs1, ve1_sb, rs1_sb)
                hidden_lo(b, 2)
                if not first:
                    pool.wait_ge(rs1_sb, b)
                head_keys(b, 2, (hi_part, lo_part), NJ * b + 3)
                hidden_lo(b, 3)
                head_keys(b, 3, (hi_part, lo_part), NJ * b + 4)
                hidden_lo(b, 4)
                if not final:
                    inverse_root(b + 1, ve0, rs0, ve0_sb, rs0_sb)
                for j in range(5, NJ):
                    hidden_lo(b, j)

            batch(0, True, False)
            col = [norm_w[:, s:s + 1].to_broadcast([P, H1]) for s in range(2)]
            pool.tensor_tensor(out=cosT_sb[:], in0=cosT_sb[:], in1=cosT_sb[:], op=ALU.mult).then_inc(rope_made, 1)
            pool.tensor_tensor(out=sinT_sb[:], in0=sinT_sb[:], in1=sinT_sb[:], op=ALU.mult).then_inc(rope_made, 1)
            pool.wait_ge(rope_made, 2)
            pool.tensor_tensor(out=cosT_sb[:], in0=cosT_sb[:], in1=sinT_sb[:], op=ALU.add).then_inc(rope_made, 1)
            pool.wait_ge(rope_made, 3)
            pool.tensor_tensor(out=cosT_sb[:], in0=cosT_sb[:], in1=col[0], op=ALU.mult).then_inc(rope_made, 1)
            pool.wait_ge(rope_made, 4)
            pool.tensor_tensor(out=cosT_sb[:], in0=cosT_sb[:], in1=col[1], op=ALU.mult).then_inc(rope_made, 1)
            pool.wait_ge(rope_made, 5)
            pool.tensor_scalar(out=qk_scale[:], in0=cosT_sb[:], scalar1=float(E1) ** -0.5 / CAP, scalar2=0.0,
                               op0=ALU.mult, op1=ALU.add).then_inc(rope_made, 1)
            pool.wait_ge(rope_made, 6)
            with pool.Fori(1, NB - 1) as b:
                batch(b, False, False)
            batch(NB - 1, False, True)
            t = NB - 1
            inverse_root(t, ve1, rs1, ve1_sb, rs1_sb)

            def norm_q(n, i):
                r = i % 2
                pool.wait_ge(msq_sb, n + 1)
                pool.tensor_tensor(out=rstd[:, r, :], in0=msq[:, r, :], in1=half_pow[:], op=ALU.pow).then_inc(rstd_sb, 1)
                pool.wait_ge(rstd_sb, n + 1)
                for tt in range(TT):
                    last = pool.tensor_tensor(out=qn[:, r, tt, :, :], in0=xs[:, r, tt, 0, :, :],
                                              in1=rstd[:, r, 4 * tt:4 * tt + 2].unsqueeze(2).to_broadcast([P, 2, E1]),
                                              op=ALU.mult)
                last.then_inc(qn_sb, 1)

            def mask(n, i):
                pool.wait_ge(exp1, n + 1)
                p = pT1[:, i % 2, :, :].rearrange("p h (c t) -> p h c t", c=3)[:, :, ::2, :]
                pool.tensor_tensor(out=p, in0=p, in1=tri_mul[:].unsqueeze(1).unsqueeze(1).to_broadcast([P, 2, 2, P]),
                                   op=ALU.mult).then_inc(masked1, 1)

            def unit_pair(w, first):
                for i in range(2 * NB):
                    n = 2 * NB * w + i
                    norm_q(n, i)
                    if not first or i >= 1:
                        mask(n - 1, i - 1)

            pool.wait_ge(yT0_ps, NB)
            pool.memset(v1[:].rearrange("p r t h e -> p (r t h) e")[:, :, E1:E1 + 1], 1.0).then_inc(v1_ones, 1)
            unit_pair(0, True)
            with pool.Fori(1, NU // 2) as w:
                unit_pair(w, False)
            mask(NU * NB - 1, -1)

            def four_chunks(w):
                for i in range(16):
                    m, r = 16 * w + i, i % 2
                    pool.wait_ge(z1h_sb, m + 1)
                    pool.tensor_tensor(out=z1l[:, r, :], in0=z1[:, r, :], in1=z1h[:, r, :].bitcast(F32),
                                       op=ALU.subtract).then_inc(z1l_sb, 1)

            with pool.Fori(0, NC // 4) as w:
                four_chunks(w)


def _layouts(x, W_qkv, W_o, W1, W2, W3, wq, wk, wv, wo, gate_w, w1s, w2s, w3s, w1r, w2r, w3r):
    import numpy as np
    f = np.float32

    def chunks(w):
        return w.reshape(w.shape[0] // P, P, w.shape[1]).transpose(1, 0, 2)

    qk = chunks(W_qkv[:, :2 * D].reshape(D, 2, NG, GR).transpose(0, 2, 1, 3).reshape(D, 2 * D)).reshape(P, -1)
    gate = np.zeros((D, P), f)
    gate[:, :NE] = gate_w.T
    vo = [chunks(np.ascontiguousarray(w)).reshape(P, -1) for w in (W_qkv[:, 2 * D:], W_o, gate)]
    attn = []
    for n in range(NU):
        r = slice(2 * E1 * n, 2 * E1 * (n + 1))
        both = np.concatenate([wq[r].T, wk[r].T], 1)
        attn.append(np.concatenate([chunks(both).reshape(P, -1), chunks(np.ascontiguousarray(wv[r].T)).reshape(P, -1),
                                    chunks(np.ascontiguousarray(wo[:, r].T)).reshape(P, -1)], 1))
    up = []
    for routed, shared in ((w1r, w1s), (w3r, w3s)):
        w = np.zeros((D, NC * P), f)
        w[:, :NR * P] = routed.transpose(1, 0, 2).reshape(D, NR * P)
        w[:, NR * P:NR * P + HE] = shared
        up.append(w)
    dn = np.zeros((NC * P, D), f)
    dn[:NR * P] = w2r.reshape(NR * P, D)
    dn[NR * P:NR * P + HE] = w2s
    expert_rows = np.zeros((P, NC * P), f)
    for e in range(NE):
        expert_rows[[e, NE + e], e * HE:(e + 1) * HE] = 1
    moe = []
    for n in range(NC // 2):
        c = slice(2 * P * n, 2 * P * (n + 1))
        moe.append(np.concatenate([chunks(np.ascontiguousarray(w[:, c])).reshape(P, -1) for w in up] +
                                  [chunks(dn[c]).reshape(P, -1), expert_rows[:, c]], 1))
    return dict(pack_qk=qk, pack_vo=np.concatenate(vo, 1),
                pack_w1=chunks(np.ascontiguousarray(W1.T)).reshape(P, -1),
                pack_w3=chunks(np.ascontiguousarray(W3.T)).reshape(P, -1),
                pack_w2=chunks(np.ascontiguousarray(W2.T)).reshape(P, -1),
                pack_attn=np.stack(attn), pack_moe=np.stack(moe))


def _rotations(rope_cos, rope_sin):
    import numpy as np
    return {n: np.repeat(np.asarray(v)[:H1].T, 2, axis=0) for n, v in (("rope_cosT", rope_cos), ("rope_sinT", rope_sin))}


def _constants():
    import numpy as np
    f = np.float32
    r = np.arange(P)
    hadamard = np.array([[1.0]])
    while hadamard.shape[0] < P:
        hadamard = np.block([[hadamard, hadamard], [hadamard, -hadamard]])
    slopes = f(2.0) ** (f(-8.0) / np.arange(1, H0 + 1, dtype=f))
    alibi_q, alibi_k = np.zeros((2, NG, T), f), np.zeros((2, 2, GH, T), f)
    for g in range(NG):
        alibi_q[g // 2, g] = 1
        alibi_k[g // 2, g % 2] = slopes[g * GH:(g + 1) * GH, None] * np.arange(T, dtype=f)
    head_mask = np.zeros((P, GH), f)
    for h in range(GH):
        head_mask[h * E0:(h + 1) * E0, h] = f(E0) ** f(-0.5)
    before = np.broadcast_to((np.arange(NE)[None, :] < np.arange(NE)[:, None]), (P, NE, NE))
    return dict(ident_c=np.eye(P, dtype=f), hadamard_c=hadamard.astype(f),
                tri_add_c=np.where(r[None, :] <= r[:, None], 0.0, -1e30).astype(f),
                tri_mul_c=(r[:, None] <= r[None, :]).astype(f), alibi_q_c=alibi_q.reshape(2, -1),
                alibi_k_c=alibi_k.reshape(2, -1), head_mask_c=head_mask,
                before_c=np.ascontiguousarray(before, f))


def kernel(L0_attn_x, L0_attn_W_qkv, L0_attn_W_o, L0_ffn_W1, L0_ffn_W2, L0_ffn_W3, L1_attn_wq, L1_attn_wk,
           L1_attn_wv, L1_attn_wo, L1_attn_q_norm_w, L1_attn_k_norm_w, L1_attn_rope_cos, L1_attn_rope_sin,
           L1_ffn_gate_w, L1_ffn_gate_b, L1_ffn_w1_shared, L1_ffn_w2_shared, L1_ffn_w3_shared, L1_ffn_w1_routed,
           L1_ffn_w2_routed, L1_ffn_w3_routed):
    import numpy as np
    import concourse.bacc as bacc
    from concourse.bass_utils import run_bass_kernel_spmd

    a = [np.asarray(v) for v in (L0_attn_x, L0_attn_W_qkv, L0_attn_W_o, L0_ffn_W1, L0_ffn_W2, L0_ffn_W3, L1_attn_wq,
                                 L1_attn_wk, L1_attn_wv, L1_attn_wo, L1_ffn_gate_w, L1_ffn_w1_shared, L1_ffn_w2_shared,
                                 L1_ffn_w3_shared, L1_ffn_w1_routed, L1_ffn_w2_routed, L1_ffn_w3_routed)]
    arrays = dict(x=a[0], **_layouts(*a), gate_b=np.asarray(L1_ffn_gate_b), q_norm=np.asarray(L1_attn_q_norm_w)[:, None],
                  k_norm=np.asarray(L1_attn_k_norm_w)[:, None], **_rotations(L1_attn_rope_cos, L1_attn_rope_sin),
                  **_constants())
    arrays = {k: np.ascontiguousarray(v) for k, v in arrays.items()}
    nc = bacc.Bacc("TRN2", target_bir_lowering=False, num_devices=1)
    aps = {k: nc.dram_tensor(k + "_dram", v.shape, F32, kind="ExternalInput").ap() for k, v in arrays.items()}
    out = nc.dram_tensor("out_dram", (NB, T, D), F32, kind="ExternalOutput").ap()
    build(nc, **aps, out=out)
    r = run_bass_kernel_spmd(nc, [{k + "_dram": v for k, v in arrays.items()}], core_ids=[0])
    return r.results[0]["out_dram"]
```
